# Optimizing a Trainium2 kernel written in Bass

```python
import numpy as np
import jax
import jax.numpy as jnp

def _softmax(x, axis=-1):
    return jax.nn.softmax(x, axis=axis)

def _gelu(x):
    return jax.nn.gelu(x, approximate=True)

def _silu(x):
    return jax.nn.silu(x)

def _sigmoid(x):
    return jax.nn.sigmoid(x)

def _layernorm(x, axis=-1, eps=1e-05):
    m = jnp.mean(x, axis=axis, keepdims=True)
    v = jnp.var(x, axis=axis, keepdims=True)
    return (x - m) / jnp.sqrt(v + eps)

def _scatter_add(tgt, idx, src, axis=0):
    return tgt.at[idx].add(src)

def _segment_sum(src, seg, n):
    return jax.ops.segment_sum(src, seg, n)
kernel_name = 'mk_gnn_resnorm_d4_gnn_r8_887f20'

def setup_inputs(seed: int=0):
    np.random.seed(seed)
    _w = jnp.asarray

    def _rec_inputs():
        import jax
        import jax.numpy as jnp
        _gk = jax.random.key(seed)
        x = -0.0004776 + 1.001 * jax.random.normal(jax.random.fold_in(_gk, 1), (1250, 1024), jnp.float32)
        _s = jax.random.randint(jax.random.fold_in(_gk, 2), (10000,), 0, 1250, jnp.int32)
        _d = jax.random.randint(jax.random.fold_in(_gk, 3), (10000,), 0, 1250, jnp.int32)
        _loop = jnp.arange(1250, dtype=jnp.int32)
        src = jnp.concatenate([_s, _d, _loop])
        dst = jnp.concatenate([_d, _s, _loop])
        _o = jnp.argsort(dst, stable=True)
        src = src[_o]
        dst = dst[_o]
        return (x, src, dst)
    x, src, dst = _rec_inputs()

    def _L0_gnn_setup():
        import jax, jax.numpy as jnp
        import numpy as np
        N_DIM = 1024
        NHID = 512
        NUM_K = 4
        DIA_LEN = [50] * 60
        N_NODES = sum(DIA_LEN)

        def _build_edge_index(dia_len):
            pieces = []
            off = 0
            for L in dia_len:
                idx = np.arange(off, off + L)
                src = np.repeat(idx, L)
                dst = np.tile(idx, L)
                m = src != dst
                pieces.append(np.stack([src[m], dst[m]], axis=0))
                off += L
            return np.concatenate(pieces, axis=1).astype(np.int32)

        def _graph_gcn(x, row, col, gw, gb, n_nodes):
            deg = jax.ops.segment_sum(jnp.ones(row.shape[0], x.dtype), col, num_segments=n_nodes)
            dis = jnp.maximum(deg, 1.0) ** (-0.5)
            norm = dis[row] * dis[col]
            x_i = x[col]
            x_j = x[row]
            alpha = jnp.tanh(x_i @ gw[:x.shape[1]] + x_j @ gw[x.shape[1]:] + gb)
            msg = norm[:, None] * alpha * x_j
            return jax.ops.segment_sum(msg, col, num_segments=n_nodes)
        key = jax.random.key(seed)
        ks = jax.random.split(key, 6)
        emotions_feat = jax.random.normal(ks[0], (N_NODES, N_DIM), dtype=jnp.float32)
        qmask = jax.random.uniform(ks[1], (max(DIA_LEN), len(DIA_LEN), 2), dtype=jnp.float32)
        edge_index = jnp.asarray(_build_edge_index(DIA_LEN))
        s1 = 1.0 / np.sqrt(N_DIM)
        W1 = jax.random.uniform(ks[2], (N_DIM, NHID), minval=-s1, maxval=s1, dtype=jnp.float32)
        b1 = jax.random.uniform(ks[3], (NHID,), minval=-s1, maxval=s1, dtype=jnp.float32)
        s2 = 1.0 / np.sqrt(2 * NHID)
        gate_w = jax.random.uniform(ks[4], (NUM_K, 2 * NHID, 1), minval=-s2, maxval=s2, dtype=jnp.float32)
        gate_b = jax.random.uniform(ks[5], (NUM_K, 1), minval=-s2, maxval=s2, dtype=jnp.float32)
        return {'emotions_feat': emotions_feat, 'qmask': qmask, 'edge_index': edge_index, 'epoch': 0, 'W1': W1, 'b1': b1, 'gate_w': gate_w, 'gate_b': gate_b}
    _L0_gnn_all = _L0_gnn_setup()
    _L0_gnn_in = {k: v for k, v in _L0_gnn_all.items() if k in ('qmask', 'W1', 'b1', 'gate_w', 'gate_b')}
    del _L0_gnn_all

    def _L1_gnn_setup():
        import jax, jax.numpy as jnp
        import numpy as np
        N_NODES = 3125
        N_EDGES = 50000
        D = 1024

        def _sage_layer(h, edge_src, edge_dst, deg_inv, W_self, W_neigh, b):
            msg = h[edge_src]
            agg = jax.ops.segment_sum(msg, edge_dst, num_segments=h.shape[0])
            mean = agg * deg_inv[:, None]
            return h @ W_self + mean @ W_neigh + b
        key = jax.random.key(seed)
        ks = jax.random.split(key, 8)
        s = 1.0 / np.sqrt(D)
        return {'x': jax.random.normal(ks[0], (N_NODES, D), dtype=jnp.float32), 'edge_src': jax.random.randint(ks[1], (N_EDGES,), 0, N_NODES, dtype=jnp.int32), 'edge_dst': jax.random.randint(ks[2], (N_EDGES,), 0, N_NODES, dtype=jnp.int32), 'W_self0': jax.random.normal(ks[3], (D, D), dtype=jnp.float32) * s, 'W_neigh0': jax.random.normal(ks[4], (D, D), dtype=jnp.float32) * s, 'b0': jnp.zeros((D,), dtype=jnp.float32), 'W_self1': jax.random.normal(ks[5], (D, D), dtype=jnp.float32) * s, 'W_neigh1': jax.random.normal(ks[6], (D, D), dtype=jnp.float32) * s, 'b1': jnp.zeros((D,), dtype=jnp.float32)}
    _L1_gnn_all = _L1_gnn_setup()
    _L1_gnn_in = {k: v for k, v in _L1_gnn_all.items() if k in ('W_self0', 'W_neigh0', 'b0', 'W_self1', 'W_neigh1', 'b1')}
    del _L1_gnn_all

    def _L2_gnn_setup():
        import jax, jax.numpy as jnp
        import numpy as np
        NEG_SLOPE = 0.1
        EPS = 1e-05
        key = jax.random.key(seed)
        k1, k2, k3, k4, k5 = jax.random.split(key, 5)
        N, E, DIN, DOUT = (1250, 20000, 1024, 1024)
        x = jax.random.normal(k1, (N, DIN), dtype=jnp.float32)
        W = jax.random.normal(k2, (DIN, DOUT), dtype=jnp.float32) * 0.02
        a = jax.random.normal(k3, (1, 2 * DOUT), dtype=jnp.float32) * 0.02
        src = jax.random.randint(k4, (E,), 0, N, dtype=jnp.int64)
        dst = jax.random.randint(k5, (E,), 0, N, dtype=jnp.int64)
        return {'x': x, 'W': W, 'a': a, 'src': src, 'dst': dst}
    _L2_gnn_all = _L2_gnn_setup()
    _L2_gnn_in = {k: v for k, v in _L2_gnn_all.items() if k in ('W', 'a')}
    del _L2_gnn_all

    def _L3_gnn_setup():
        import jax, jax.numpy as jnp
        import numpy as np
        N_NODES = 1250
        N_EDGES = 20000
        DIM = 1024
        key = jax.random.key(seed)
        k1, k2, k3 = jax.random.split(key, 3)
        x = jax.random.normal(k1, (N_NODES, DIM), dtype=jnp.float32)
        edge_index = jax.random.randint(k2, (2, N_EDGES), 0, N_NODES, dtype=jnp.int64)
        W = jax.random.normal(k3, (DIM, DIM), dtype=jnp.float32) * (1.0 / np.sqrt(DIM))
        b = jnp.zeros((DIM,), dtype=jnp.float32)
        return {'x': x, 'edge_index': edge_index, 'W': W, 'b': b}
    _L3_gnn_all = _L3_gnn_setup()
    _L3_gnn_in = {k: v for k, v in _L3_gnn_all.items() if k in ('W', 'b')}
    del _L3_gnn_all
    return {'x': x, 'src': src, 'dst': dst, 'L0_gnn_qmask': _L0_gnn_in['qmask'], 'L0_gnn_W1': _L0_gnn_in['W1'], 'L0_gnn_b1': _L0_gnn_in['b1'], 'L0_gnn_gate_w': _L0_gnn_in['gate_w'], 'L0_gnn_gate_b': _L0_gnn_in['gate_b'], 'L1_gnn_W_self0': _L1_gnn_in['W_self0'], 'L1_gnn_W_neigh0': _L1_gnn_in['W_neigh0'], 'L1_gnn_b0': _L1_gnn_in['b0'], 'L1_gnn_W_self1': _L1_gnn_in['W_self1'], 'L1_gnn_W_neigh1': _L1_gnn_in['W_neigh1'], 'L1_gnn_b1': _L1_gnn_in['b1'], 'L2_gnn_W': _L2_gnn_in['W'], 'L2_gnn_a': _L2_gnn_in['a'], 'L3_gnn_W': _L3_gnn_in['W'], 'L3_gnn_b': _L3_gnn_in['b']}

def reference(x, src, dst, L0_gnn_qmask, L0_gnn_W1, L0_gnn_b1, L0_gnn_gate_w, L0_gnn_gate_b, L1_gnn_W_self0, L1_gnn_W_neigh0, L1_gnn_b0, L1_gnn_W_self1, L1_gnn_W_neigh1, L1_gnn_b1, L2_gnn_W, L2_gnn_a, L3_gnn_W, L3_gnn_b):
    import jax
    import jax.numpy as jnp

    def _L0_gnn_ref(emotions_feat, qmask, edge_index, epoch, W1, b1, gate_w, gate_b):
        import jax, jax.numpy as jnp
        import numpy as np
        N_DIM = 1024
        NHID = 512
        NUM_K = 4
        DIA_LEN = [50] * 60
        N_NODES = sum(DIA_LEN)

        def _build_edge_index(dia_len):
            pieces = []
            off = 0
            for L in dia_len:
                idx = np.arange(off, off + L)
                src = np.repeat(idx, L)
                dst = np.tile(idx, L)
                m = src != dst
                pieces.append(np.stack([src[m], dst[m]], axis=0))
                off += L
            return np.concatenate(pieces, axis=1).astype(np.int32)

        def _graph_gcn(x, row, col, gw, gb, n_nodes):
            deg = jax.ops.segment_sum(jnp.ones(row.shape[0], x.dtype), col, num_segments=n_nodes)
            dis = jnp.maximum(deg, 1.0) ** (-0.5)
            norm = dis[row] * dis[col]
            x_i = x[col]
            x_j = x[row]
            alpha = jnp.tanh(x_i @ gw[:x.shape[1]] + x_j @ gw[x.shape[1]:] + gb)
            msg = norm[:, None] * alpha * x_j
            return jax.ops.segment_sum(msg, col, num_segments=n_nodes)
        row, col = (edge_index[0], edge_index[1])
        n_nodes = emotions_feat.shape[0]
        x1 = emotions_feat @ W1 + b1
        gnn_out = x1
        for kk in range(NUM_K):
            gnn_out = gnn_out + _graph_gcn(gnn_out, row, col, gate_w[kk], gate_b[kk], n_nodes)
        return jnp.concatenate([x1, gnn_out], axis=1)

    def _L1_gnn_ref(x, edge_src, edge_dst, W_self0, W_neigh0, b0, W_self1, W_neigh1, b1):
        import jax, jax.numpy as jnp
        import numpy as np
        N_NODES = 3125
        N_EDGES = 50000
        D = 1024

        def _sage_layer(h, edge_src, edge_dst, deg_inv, W_self, W_neigh, b):
            msg = h[edge_src]
            agg = jax.ops.segment_sum(msg, edge_dst, num_segments=h.shape[0])
            mean = agg * deg_inv[:, None]
            return h @ W_self + mean @ W_neigh + b
        N = x.shape[0]
        deg = jax.ops.segment_sum(jnp.ones_like(edge_dst, dtype=x.dtype), edge_dst, num_segments=N)
        deg_inv = 1.0 / jnp.maximum(deg, 1.0)
        h = jax.nn.relu(_sage_layer(x, edge_src, edge_dst, deg_inv, W_self0, W_neigh0, b0))
        out = _sage_layer(h, edge_src, edge_dst, deg_inv, W_self1, W_neigh1, b1)
        return out

    def _L2_gnn_ref(x, W, a, src, dst):
        import jax, jax.numpy as jnp
        import numpy as np
        NEG_SLOPE = 0.1
        EPS = 1e-05
        N = x.shape[0]
        d = W.shape[1]
        h = x @ W
        a_l, a_r = (a[0, :d], a[0, d:])
        al = h @ a_l
        ar = h @ a_r
        e = jnp.exp(-jax.nn.leaky_relu(al[src] + ar[dst], negative_slope=NEG_SLOPE))
        rowsum = jax.ops.segment_sum(e, src, num_segments=N)
        h_prime = jax.ops.segment_sum(e[:, None] * h[dst], src, num_segments=N)
        h_prime = h_prime / (rowsum[:, None] + EPS)
        return jax.nn.elu(h_prime)

    def _L3_gnn_ref(x, edge_index, W, b):
        import jax, jax.numpy as jnp
        import numpy as np
        N_NODES = 1250
        N_EDGES = 20000
        DIM = 1024
        'GCNConv (add_self_loops=True, symmetric norm) -> Dropout(eval=identity) -> ReLU.'
        n = x.shape[0]
        loops = jnp.arange(n, dtype=edge_index.dtype)
        src = jnp.concatenate([edge_index[0], loops])
        dst = jnp.concatenate([edge_index[1], loops])
        deg = jax.ops.segment_sum(jnp.ones_like(dst, dtype=x.dtype), dst, num_segments=n)
        dinv = jnp.where(deg > 0, jax.lax.rsqrt(deg), jnp.zeros_like(deg))
        norm = dinv[src] * dinv[dst]
        h = x @ W
        msg = h[src] * norm[:, None]
        out = jax.ops.segment_sum(msg, dst, num_segments=n) + b
        return jax.nn.relu(out)
    edge_index = jnp.stack([src, dst])
    x = _layernorm(x + _L0_gnn_ref(x, L0_gnn_qmask, edge_index, 0, L0_gnn_W1, L0_gnn_b1, L0_gnn_gate_w, L0_gnn_gate_b), axis=-1)
    x = _layernorm(x + _L1_gnn_ref(x, src, dst, L1_gnn_W_self0, L1_gnn_W_neigh0, L1_gnn_b0, L1_gnn_W_self1, L1_gnn_W_neigh1, L1_gnn_b1), axis=-1)
    x = _layernorm(x + _L2_gnn_ref(x, L2_gnn_W, L2_gnn_a, src, dst), axis=-1)
    x = _layernorm(x + _L3_gnn_ref(x, edge_index, L3_gnn_W, L3_gnn_b), axis=-1)
    return x

_drawn_inputs = setup_inputs


def setup_inputs(seed=0):
    import zlib

    import numpy as np

    out = dict(_drawn_inputs(seed))
    spreads = {'L1_gnn_b0': (0.0, 0.1), 'L1_gnn_b1': (0.0, 0.1), 'L3_gnn_b': (0.0, 0.1)}
    factors = {'L0_gnn_gate_b': 64.0}
    for name, (base, spread) in spreads.items():
        noise = np.random.default_rng([zlib.crc32(name.encode()), seed]).standard_normal(out[name].shape)
        drawn = base * np.exp(spread * noise) if base else spread * noise
        out[name] = jnp.asarray(drawn.astype(out[name].dtype))
    for name, factor in factors.items():
        out[name] = (out[name] * factor).astype(out[name].dtype)
    return out
```

```python
import numpy as np
import concourse.bass as bass
from concourse import mybir
from contextlib import ExitStack

N, D, E = 1250, 1024, 21250
T = 125
NT = N // T
NC = E // T
HW = 512
PER = NC // NT
MARGIN = 3
NSLOT = 11


def windows():
    out = []
    for c in range(NC):
        lo = max(0, -((PER - 1 + MARGIN - c) // PER))
        hi = min(NT - 1, (c + MARGIN) // PER)
        out.append((lo, hi))
    return out


class Queue:

    def __init__(self, sem):
        self.sem, self.n, self.items = sem, 0, []

    def op(self, fn, *waits):
        self.n += 1
        self.items.append((fn, waits, (self.sem, 1)))
        return (self.sem, self.n)

    def quiet(self, fn, *waits):
        self.items.append((fn, waits, None))

    def wait(self, *waits):
        self.items.append((None, waits, None))

    def emit(self, eng):
        seen = {}
        for fn, waits, inc in self.items:
            for w in waits:
                if w is None:
                    continue
                sem, v = w
                if seen.get(id(sem), 0) < v:
                    eng.wait_ge(sem, v)
                    seen[id(sem)] = v
            if fn is None:
                continue
            ins = fn()
            if inc is not None:
                ins.then_inc(*inc)


class Slot:

    def __init__(self, sem):
        self.sem, self.n = sem, 0

    def dma(self, q, eng, out, in_, *waits):
        self.n += 16
        q.items.append((lambda: eng.dma_start(out, in_), waits, (self.sem, 16)))
        return (self.sem, self.n)


class Job:
    def __init__(self, mm, prep=None, post=None, tail=None, after=-1, w=None, late=None):
        self.late = late
        self.mm, self.prep, self.post, self.tail, self.after, self.w = mm, prep, post, tail, after, w


def gnn_program(nc, xT, x, es, ed, win, W1, b1, gw, gb, Ws0, Wn0, b0, Ws1, Wn1, bb1, W2, a2, W3, b3, out):
    f32, fr, bf, f16 = mybir.dt.float32, mybir.dt.float32r, mybir.dt.bfloat16, mybir.dt.float16
    i16, i32 = mybir.dt.int16, mybir.dt.int32
    ALU, ACT = mybir.AluOpType, mybir.ActivationFunctionType
    AXX = mybir.AxisListType.X
    FMAX = 3.0e38

    def dram(name, shape, dt):
        return nc.dram_tensor(name, shape, dt, kind="Internal").ap()

    a_d = dram("a_d", (NT, T, NT * T), i16)
    at_d = dram("at_d", (NT, T, NT * T), i16)
    x_d = [dram(f"x_d{i}", (NT, T, D), f32) for i in range(3)]
    xT_d = [xT] + [dram(f"xT_d{i}", (NT, 128, 8 * T), f32) for i in range(1, 4)]
    hT_d = dram("hT_d", (NT, 128, 8 * T), f32)
    yl_d = dram("yl_d", (NT, T, HW), f32)

    ctx = ExitStack()
    with ctx:
        def sb(name, shape, dt, c=None):
            return (c or ctx).enter_context(nc.sbuf_tensor(name, shape, dt))

        def sem(name):
            return ctx.enter_context(nc.semaphore(name))

        PE, V, A, P, S = (Queue(sem(f"q_{n}")) for n in ("pe", "dve", "act", "pool", "sync"))
        te, ve, ac, po, sy = nc.tensor, nc.vector, nc.scalar, nc.gpsimd, nc.sync

        wh = [sb(f"wh{i}", [128, HW], fr) for i in range(NSLOT)]
        wl = [sb(f"wl{i}", [128, HW], fr) for i in range(NSLOT)]
        ws = [sb(f"ws{i}", [128, HW], f32) for i in range(2)]
        xs = [sb(f"xs{i}", [128, 8, T], f32) for i in range(2)]
        xh = [sb(f"xh{i}", [128, 8, T], fr) for i in range(2)]
        xl = [sb(f"xl{i}", [128, 8, T], fr) for i in range(2)]
        ident = sb("ident", [128, 128], f32)
        ones = sb("ones", [128, 4], f32)
        onesr = sb("onesr", [128, 2], fr)
        DEG = sb("DEG", [T, NT], f32)
        DIS = sb("DIS", [T, NT], f32)
        DEGI = sb("DEGI", [T, NT], f32)
        D3 = sb("D3", [T, NT], f32)
        sm = sb("sm", [128, 16], f32)
        flags = sb("flags", [1, 2], i32)
        WC = sb("WC", [128, 2, 8], f32)
        GB = sb("GB", [128, 4], f32)
        PQ = [[sb(f"P{i}", [T, NT], f32), sb(f"Q{i}", [T, NT], f32)] for i in range(2)]
        RS = sb("RS", [T, NT], f32)
        st = [sb(f"st{i}", [T, 12], f32) for i in range(2)]
        mv = [sb(f"mv{i}", [T, 4], f32) for i in range(2)]
        bank = [ctx.enter_context(nc.psum_tensor(f"bank{i}", [128, HW], f32)) for i in range(8)]
        bank_free = [None] * 8
        turn = [0]

        def take():
            b = turn[0] % 6
            turn[0] += 1
            return b

        halves = []
        wsl = [Slot(sem(f"s_ws{i}")) for i in range(2)]
        ws_free = [(), ()]
        slot_free = [()] * NSLOT
        w_tok = {}
        nslab = [0]

        def add_half(ap):
            halves.append(ap)
            return len(halves) - 1

        def load_slab():
            g = nslab[0]
            nslab[0] += 1
            h, k = divmod(g, 8)
            i, s = g % 2, g % NSLOT
            t = wsl[i].dma(S, sy, ws[i][:], halves[h][k * 128:(k + 1) * 128, :], *ws_free[i])
            th = A.op(lambda: ac.copy(wh[s][:], ws[i][:]), t, *slot_free[s])
            tl = P.op(lambda: po.tensor_tensor(wl[s][:], ws[i][:], wh[s][:].bitcast(f32), ALU.subtract), t, th,
                      *slot_free[s])
            ws_free[i] = (tl,)
            w_tok[h, k] = (s, th, tl)

        def may_load(done):
            while nslab[0] < 8 * len(halves) and (nslab[0] < NSLOT or (nslab[0] - NSLOT) // 8 <= done):
                load_slab()

        xsl = [Slot(sem(f"s_xs{i}")) for i in range(2)]
        x_turn = [0]
        xs_free = [(), ()]
        x_free = [None, None]

        def prep_x(src, ready):
            def prep(box):
                i = x_turn[0] % 2
                x_turn[0] += 1
                t = xsl[i].dma(S, sy, xs[i][:], src.rearrange("p (k n) -> p k n", k=8), *xs_free[i], *ready())
                th = A.op(lambda: ac.copy(xh[i][:], xs[i][:]), t, x_free[i])
                tl = V.op(lambda: ve.tensor_tensor(xl[i][:], xs[i][:], xh[i][:].bitcast(f32), ALU.subtract), t, th,
                          x_free[i])
                xs_free[i] = (tl,)
                box["x"] = (i, th, tl)
            return prep

        def mm_x(h):
            def mm(box):
                i, th, tl = box["x"]
                b = take()
                PE.wait(th, tl, bank_free[b])
                for k in range(8):
                    s, wth, wtl = w_tok[h, k]
                    PE.wait(wth, wtl)
                    o = bank[b][0:T, :]
                    PE.quiet(lambda k=k, s=s: te.matmul(o, xh[i][:, k, :], wh[s][:], start=(k == 0), stop=False))
                    PE.quiet(lambda k=k, s=s: te.matmul(o, xh[i][:, k, :], wl[s][:], start=False, stop=False))
                    f = (lambda k=k, s=s: te.matmul(o, xl[i][:, k, :], wh[s][:], start=False, stop=(k == 7)))
                    if k < 7:
                        PE.quiet(f)
                t = PE.op(f)
                x_free[i] = t
                for k in range(8):
                    slot_free[w_tok[h, k][0]] = (t,)
                box["b"], box["t"] = b, t
            return mm

        hW1 = add_half(W1)
        for wn, wsf in ((Wn0, Ws0), (Wn1, Ws1)):
            for f in range(2):
                add_half(wn[:, f * HW:(f + 1) * HW])
                add_half(wsf[:, f * HW:(f + 1) * HW])
        for w in (W2, W3):
            for f in range(2):
                add_half(w[:, f * HW:(f + 1) * HW])

        WIN = windows()
        first = {b: min(c for c in range(NC) if WIN[c][0] <= b <= WIN[c][1]) for b in range(NT)}
        last = {b: max(c for c in range(NC) if WIN[c][0] <= b <= WIN[c][1]) for b in range(NT)}
        PC = [(0, 417), (417, 834), (834, 1250)]

        ca = ExitStack()
        ei = sb("ei", [T, 2, NC], i32, ca)
        ef = sb("ef", [T, 2, NC], f32, ca)
        wn_ = sb("wn_", [T, 2, NC], f32, ca)
        wt = sb("wt", [T, 2, NC], f32, ca)
        iot = sb("iot", [T, N], f16, ca)
        oS = [sb(f"oS{i}", [T, N], bf, ca) for i in range(4)]
        oD = [sb(f"oD{i}", [T, 2 * T], bf, ca) for i in range(4)]
        zz = sb("zz", [T, HW], bf, ca)
        AT = sb("AT", [T, NT, N], i16, ca)
        Af = [sb(f"Af{i}", [T, N], f32, ca) for i in range(2)]
        A16 = [sb(f"A16{i}", [T, NT, T], i16, ca) for i in range(2)]
        aB = sb("aB", [128, 2 * D], f32, ca)
        w2r = [sb(f"w2r{i}", [128, D], f32, ca) for i in range(2)]
        w2t = sb("w2t", [128, D], f32, ca)
        ca.close()

        s_e, s_c = Slot(sem("s_e")), Slot(sem("s_c"))
        te_ = s_e.dma(S, sy, ei[:, 0, :], es)
        te_ = s_e.dma(S, sy, ei[:, 1, :], ed)
        te_ = s_e.dma(S, sy, wn_[:], win.rearrange("p (a c) -> p a c", a=2))
        tc_ = s_c.dma(S, sy, GB[:], gb.rearrange("k o -> o k").partition_broadcast(128).rearrange("p o k -> p (o k)"))
        tc_ = s_c.dma(S, sy, aB[:], a2.partition_broadcast(128).rearrange("p o k -> p (o k)"))

        ti = P.op(lambda: po.iota(iot[:], [[1, N]], base=0, channel_multiplier=0, allow_small_or_imprecise_dtypes=True))
        t0 = P.op(lambda: po.memset(ident[:], 0.0))
        tid = P.op(lambda: po.affine_select(out=ident[:], in_=ident[:], compare_op=ALU.not_equal, fill=1.0, base=0,
                                            pattern=[[-1, 128]], channel_multiplier=1), t0)
        to = P.op(lambda: po.memset(ones[:], 1.0))
        tz = P.op(lambda: po.memset(zz[:], 0.0))
        tor = V.op(lambda: ve.tensor_copy(onesr[:], ones[:, 0:2]), to)

        t1 = V.op(lambda: ve.tensor_copy(ef[:], ei[:]), te_)
        t2 = V.op(lambda: ve.tensor_tensor(wt[:, 0, :], wn_[:, 0, :], ef[:, 1, :], ALU.subtract), t1)
        t3 = V.op(lambda: ve.tensor_tensor(wt[:, 1, :], ef[:, 1, :], wn_[:, 1, :], ALU.subtract), t1)
        t4 = V.op(lambda: ve.reduce_max(sm[0:T, 0:1], wt[:].rearrange("p a c -> p (a c)"), AXX), t2, t3)
        t5 = V.op(lambda: ve.tensor_scalar(sm[0:T, 1:2], sm[0:T, 0:1], 0.0, None, ALU.is_gt), t4)
        t6 = PE.op(lambda: te.matmul(bank[7][0:1, 0:1], sm[0:T, 1:2], ones[0:T, 0:1], start=True, stop=True), t5, to)
        tflag = V.op(lambda: ve.tensor_copy(flags[0:1, 0:1], bank[7][0:1, 0:1]), t6)

        may_load(-1)

        fS, fP, fE = sem("fS"), sem("fP"), sem("fE")
        gS, gP, gB, gE = sem("gS"), sem("gP"), sem("gB"), sem("gE")
        eng_of = {id(PE): te, id(V): ve, id(A): ac}

        def one_hots(c, i, col):
            ve.tensor_scalar(oS[i][:], iot[:], ef[:, 0, col], None, ALU.is_equal).then_inc(*c)

        def dve_build():
            v = ve.value_load(flags[0:1, 0:1], min_val=0, max_val=T)
            with ve.If(v < 1):
                for c in range(NC):
                    i = c % 4
                    lo, hi = WIN[c]
                    if c >= 4:
                        ve.wait_ge(fP, c - 3)
                    ve.tensor_scalar(oS[i][:], iot[:], ef[:, 0, c:c + 1], None, ALU.is_equal).then_inc(fS, 1)
                    n = (hi - lo + 1) * T
                    ve.tensor_scalar(oD[i][:, 0:n], iot[:, lo * T:lo * T + n], ef[:, 1, c:c + 1], None,
                                     ALU.is_equal).then_inc(fS, 1)
            with ve.Else():
                for b in range(NT):
                    with ve.Fori(0, NC) as c:
                        ve.wait_ge(gP, 1)
                        ve.sem_clear(gP)
                        ve.tensor_scalar(oS[0][:], iot[:], ef[:, 0, bass.ds(c, 1)], None, ALU.is_equal).then_inc(gS, 1)
                        ve.tensor_scalar(oD[0][:, 0:T], iot[:, b * T:(b + 1) * T], ef[:, 1, bass.ds(c, 1)], None,
                                         ALU.is_equal).then_inc(gS, 1)

        def pe_build():
            v = te.value_load(flags[0:1, 0:1], min_val=0, max_val=T)
            with te.If(v < 1):
                for c in range(NC):
                    i = c % 4
                    lo, hi = WIN[c]
                    te.wait_ge(fS, 2 * (c + 1))
                    for b in range(lo, hi + 1):
                        if c == first[b] and b >= 2:
                            te.wait_ge(fE, b - 1)
                        for j, (u, w) in enumerate(PC):
                            m = te.matmul(bank[3 * (b % 2) + j][0:T, 0:w - u], oD[i][:, (b - lo) * T:(b - lo + 1) * T],
                                          oS[i][:, u:w], start=(c == first[b]), stop=(c == last[b]))
                    m.then_inc(fP, 1)
            with te.Else():
                te.sem_inc(gP, 1)
                for b in range(NT):
                    if b:
                        te.wait_ge(gE, b)
                    for j, (u, w) in enumerate(PC):
                        te.matmul(bank[j][0:T, 0:w - u], zz[:, 0:T], zz[:, 0:w - u], start=True, stop=False)
                    with te.Fori(0, NC) as c:
                        te.wait_ge(gS, 2)
                        te.sem_clear(gS)
                        for j, (u, w) in enumerate(PC):
                            m = te.matmul(bank[j][0:T, 0:w - u], oD[0][:, 0:T], oS[0][:, u:w], start=False, stop=False)
                        m.then_inc(gP, 1)
                    for j, (u, w) in enumerate(PC):
                        m = te.matmul(bank[j][0:T, 0:w - u], zz[:, 0:T], zz[:, 0:w - u], start=False, stop=True)
                    m.then_inc(gB, 1)

        def act_build():
            v = ac.value_load(flags[0:1, 0:1], min_val=0, max_val=T)
            with ac.If(v < 1):
                for b in range(NT):
                    ac.wait_ge(fP, last[b] + 1)
                    for j, (u, w) in enumerate(PC):
                        m = ac.copy(AT[:, b, u:w], bank[3 * (b % 2) + j][0:T, 0:w - u])
                    m.then_inc(fE, 1)
            with ac.Else():
                for b in range(NT):
                    ac.wait_ge(gB, b + 1)
                    for j, (u, w) in enumerate(PC):
                        m = ac.copy(AT[:, b, u:w], bank[j][0:T, 0:w - u])
                    m.then_inc(gE, 1)

        V.wait(t1, ti, tflag)
        V.quiet(lambda: (dve_build(), None)[1])
        PE.wait(tz, tflag)
        PE.quiet(lambda: (pe_build(), None)[1])
        A.wait(tflag)
        A.quiet(lambda: (act_build(), None)[1])
        tA = A.op(lambda: ac.copy(sm[0:1, 8:9], ident[0:1, 0:1]), tid)
        tPE = PE.op(lambda: te.matmul(bank[7][0:1, 0:1], ones[0:1, 0:1], ones[0:1, 0:1], start=True, stop=True), tflag)
        for b in range(8):
            bank_free[b] = tA

        sw = [Slot(sem(f"s_w2{i}")) for i in range(2)]
        w2f = [None, None]
        for k in range(8):
            i = k % 2
            t = sw[i].dma(S, sy, w2r[i][:], W2[k * 128:(k + 1) * 128, :], w2f[i])
            for j in range(2):
                w2f[i] = V.op(lambda k=k, j=j, i=i: ve.tensor_tensor_reduce(
                    out=w2t[:], in0=w2r[i][:], in1=aB[:, j * D:(j + 1) * D], scale=1.0, scalar=0.0,
                    op0=ALU.mult, op1=ALU.add, accum_out=WC[:, j, k:k + 1]), t, tc_, (V.sem, V.n))
        tWC = w2f[1]

        s_at = Slot(sem("s_at"))
        s_a = [Slot(sem(f"s_a{i}")) for i in range(2)]
        tat = s_at.dma(S, sy, at_d.rearrange("t p (b s) -> p b t s", b=NT),
                       AT[:].rearrange("p b (t s) -> p b t s", t=NT), tA) if False else None
        for b in range(NT):
            tat = s_at.dma(S, sy, at_d[:, :, b * T:(b + 1) * T].rearrange("t p s -> p t s"),
                           AT[:, b, :].rearrange("p (t s) -> p t s", t=NT), tA)
        af_free = [None, None]
        a16_free = [None, None]
        a_tok = []
        for b in range(NT):
            i = b % 2
            tf = V.op(lambda b=b, i=i: ve.tensor_copy(Af[i][:], AT[:, b, :]), tA, af_free[i])
            V.op(lambda b=b, i=i: ve.reduce_sum(DEG[:, b:b + 1], Af[i][:], AXX), tf)
            evs = []
            for g, (u, w) in enumerate(((0, 4), (4, 8), (8, 10))):
                bk = 2 * (g % 2) + i if g < 2 else 4 + i
                for j in range(u, w):
                    fn = (lambda b=b, i=i, j=j, u=u, bk=bk: te.transpose(bank[bk][0:T, (j - u) * T:(j - u + 1) * T],
                                                                       Af[i][:, j * T:(j + 1) * T], ident[0:T, 0:T]))
                    tt = PE.op(fn, tf, bank_free[bk], tid)
                ev = A.op(lambda i=i, u=u, w=w, bk=bk: ac.copy(
                    A16[i][:, u:w, :], bank[bk][0:T, 0:(w - u) * T].rearrange("p (a c) -> p a c", c=T)), tt, a16_free[i])
                bank_free[bk] = ev
            af_free[i] = tt
            a16_free[i] = s_a[i].dma(S, sy, a_d[b].rearrange("p (a c) -> p a c", c=T), A16[i][:], ev)
            a_tok.append(a16_free[i])
        dd = (V.sem, V.n)
        t = V.op(lambda: ve.tensor_scalar(DEGI[:], DEG[:], 1.0, None, ALU.max), dd)
        t = V.op(lambda: ve.reciprocal(DEGI[:], DEGI[:]), t)
        t = V.op(lambda: ve.tensor_scalar(D3[:], DEG[:], 1.0, None, ALU.add), dd, t)
        t = V.op(lambda: ve.reciprocal(D3[:], D3[:]), t)
        u1 = A.op(lambda: ac.activation(DIS[:], DEGI[:], ACT.Sqrt), t)
        u2 = A.op(lambda: ac.activation(D3[:], D3[:], ACT.Sqrt), t)
        tdeg = u2
        t = V.op(lambda: ve.reduce_max(sm[0:T, 2:3], DEG[:], AXX), dd)
        t = V.op(lambda: ve.tensor_scalar(sm[0:T, 3:4], sm[0:T, 2:3], 4096.0, None, ALU.is_gt), t)
        t = PE.op(lambda: te.matmul(bank[7][0:1, 0:1], sm[0:T, 3:4], ones[0:T, 0:1], start=True, stop=True), t)
        tbig = V.op(lambda: ve.tensor_copy(flags[0:1, 1:2], bank[7][0:1, 0:1]), t)
        bank_free[7] = tbig
        big = {}
        PE.quiet(lambda: big.update(v=te.value_load(flags[0:1, 1:2], min_val=0, max_val=T)), tbig)

        ends = [(PE.sem, PE.n), (V.sem, V.n), (A.sem, A.n), (P.sem, P.n), tat, a_tok[-1], a_tok[-2]]
        for q in (PE, V, A, P, S):
            q.wait(*ends)

        Zh = sb("Zh", [T, NT, HW], fr)
        Zl = sb("Zl", [T, NT, HW], fr)
        G = sb("G", [T, NT, HW], f32)
        Mh = [sb(f"Mh{i}", [T, NT, T], fr) for i in range(2)]
        Ml = [sb(f"Ml{i}", [T, NT, T], fr) for i in range(2)]
        Tt = [sb(f"Tt{i}", [T, NT, T], f32) for i in range(2)]
        Ar = [sb(f"Ar{i}", [T, NT, T], i16) for i in range(3)]
        PB = sb("PB", [T, NT, T], f32)
        GW = sb("GW", [128, 2, D], f32)
        R = [sb(f"R{i}", [T, HW], f32) for i in range(4)]
        U = [sb(f"U{i}", [T, HW], f32) for i in range(2)]
        XO = sb("XO", [T, D], f32)
        XT = sb("XT", [128, 8, T], f32)
        B = sb("B", [128, HW], f32)

        jobs = []
        s_gw = [Slot(sem(f"s_gw{i}")) for i in range(2)]
        s_ar = [Slot(sem(f"s_ar{i}")) for i in range(3)]
        s_r = [Slot(sem(f"s_r{i}")) for i in range(4)]
        s_b = Slot(sem("s_b"))
        s_xo, s_xt, s_u = Slot(sem("s_xo")), Slot(sem("s_xt")), [Slot(sem(f"s_u{i}")) for i in range(2)]
        free = {"gw": [None, None], "ar": [None] * 3, "r": [None] * 4, "u": [None] * 2, "t": [None] * 2,
                "m": [None] * 2, "xo": None, "xt": None, "b": None, "pb": None, "st": [None] * 2}
        cnt = {"ar": 0, "r": 0, "u": 0, "t": 0, "st": 0}
        tok = {}

        def nxt(name, n):
            i = cnt[name] % n
            cnt[name] += 1
            return i

        def load_r(src, *waits):
            i = nxt("r", 4)
            return i, s_r[i].dma(S, sy, R[i][:], src, free["r"][i], *waits)

        def load_b(src):
            tok["b"] = s_b.dma(S, sy, B[:], src.rearrange("(o c) -> o c", o=1).partition_broadcast(128).rearrange("p o c -> p (o c)"), free["b"])

        def prep_m(kind, d, par=0):
            def prep(box):
                r = nxt("ar", 3)
                src = at_d if kind == "att" else a_d
                ta = s_ar[r].dma(S, sy, Ar[r][:], src[d].rearrange("p (a c) -> p a c", c=T), free["ar"][r])
                i = nxt("t", 2)
                if kind in ("gate", "att"):
                    col = PQ[par][1] if kind == "gate" else PQ[0][0]
                    row = PB[:, d, :].unsqueeze(1).to_broadcast([T, NT, T])
                    cb = col[:].unsqueeze(2).to_broadcast([T, NT, T])
                    t = P.op(lambda: po.tensor_tensor(Tt[i][:], row, cb, ALU.add), free["t"][i], tok["pb"], tok["pq"])
                    free["pb"] = t
                    if kind == "gate":
                        t = A.op(lambda: ac.activation(Tt[i][:], Tt[i][:], ACT.Tanh), t)
                        t = V.op(lambda: ve.tensor_tensor(Tt[i][:], Tt[i][:], Ar[r][:], ALU.mult), t, ta)
                    else:
                        t = V.op(lambda: ve.scalar_tensor_tensor(Tt[i][:], Tt[i][:], 0.1, Tt[i][:], ALU.mult, ALU.max),
                                 t)
                        t = A.op(lambda: ac.activation(Tt[i][:], Tt[i][:], ACT.Exp, scale=-1.0), t)
                        t = V.op(lambda: ve.scalar_tensor_tensor(Tt[i][:], Tt[i][:], FMAX, Ar[r][:], ALU.min, ALU.mult),
                                 t, ta)
                    free["ar"][r] = t
                    th = A.op(lambda: ac.copy(Mh[i][:], Tt[i][:]), t, free["m"][i])
                    tl = V.op(lambda: ve.tensor_tensor(Ml[i][:], Tt[i][:], Mh[i][:].bitcast(f32), ALU.subtract), th,
                              free["m"][i])
                    free["t"][i] = tl
                else:
                    if kind == "loop":
                        ta = V.op(lambda: ve.tensor_tensor(Ar[r][:, d, :], Ar[r][:, d, :], ident[0:T, 0:T], ALU.add), ta)
                    th = A.op(lambda: ac.copy(Mh[i][:], Ar[r][:]), ta, free["m"][i])
                    tl = V.op(lambda: ve.tensor_tensor(Ml[i][:], Ar[r][:], Mh[i][:].bitcast(f32), ALU.subtract), th, ta,
                              free["m"][i])
                    free["ar"][r] = tl
                box["m"] = (i, th, tl)
            return prep

        def mm_m(kind, rowsum=False):
            def mm(box):
                i, th, tl = box["m"]
                b = take()
                o = bank[b][0:T, :]
                PE.wait(bank_free[b], th)
                full = kind in ("gate", "att")
                for s in range(NT):
                    PE.wait(*tok["z", s])
                    PE.quiet(lambda s=s: te.matmul(o, Mh[i][:, s, :], Zh[:, s, :], start=(s == 0), stop=False))
                    if full:
                        PE.quiet(lambda s=s: te.matmul(o, Mh[i][:, s, :], Zl[:, s, :], start=False, stop=False))
                        PE.wait(tl)
                        f = (lambda s=s: te.matmul(o, Ml[i][:, s, :], Zh[:, s, :], start=False, stop=(s == NT - 1)))
                    else:
                        f = (lambda s=s: te.matmul(o, Mh[i][:, s, :], Zl[:, s, :], start=False, stop=(s == NT - 1)))
                        if s == 0:
                            PE.wait(tl)

                            def extra():
                                with te.If(big["v"] > 0):
                                    for r in range(NT):
                                        te.matmul(o, Ml[i][:, r, :], Zh[:, r, :], start=False, stop=False)
                            zt = [tok["z", r] for r in range(NT)]
                            box["extra"] = (extra, zt)
                    if s < NT - 1:
                        PE.quiet(f)
                if "extra" in box:
                    PE.quiet(box["extra"][0], *[w for z in box["extra"][1] for w in z])
                t = PE.op(f)
                if rowsum:
                    rb = 7
                    for s in range(NT):
                        for m, (M, z) in enumerate(((Mh, 0), (Ml, 1))):
                            f2 = (lambda s=s, M=M, z=z: te.matmul(bank[rb][0:T, 0:2], M[i][:, s, :], onesr[0:T, :],
                                                                  start=(s == 0 and z == 0),
                                                                  stop=(s == NT - 1 and z == 1)))
                            if s == 0 and m == 0:
                                PE.wait(bank_free[rb], tor)
                            if not (s == NT - 1 and m == 1):
                                PE.quiet(f2)
                    t = PE.op(f2)
                free["m"][i] = t
                tok["magg"] = t
                box["b"], box["t"] = b, t
            return mm

        def split_z(n, src, scale, *waits):
            sc = None if scale is None else scale[:, n:n + 1]
            if sc is None:
                th = A.op(lambda: ac.copy(Zh[:, n, :], src), *waits)
                tl = V.op(lambda: ve.tensor_tensor(Zl[:, n, :], src, Zh[:, n, :].bitcast(f32), ALU.subtract), th, *waits)
            else:
                th = A.op(lambda: ac.activation(Zh[:, n, :], src, ACT.Copy, scale=sc), *waits)
                tl = V.op(lambda: ve.scalar_tensor_tensor(Zl[:, n, :], src, sc, Zh[:, n, :].bitcast(f32), ALU.mult,
                                                         ALU.subtract), th, *waits)
            tok["z", n] = (th, tl)
            return tl, th

        def norm(left, right, waits):
            i = nxt("st", 2)
            V.op(lambda: ve.bn_stats(st[i][:, 0:6], left), *waits)
            t = V.op(lambda: ve.bn_stats(st[i][:, 6:12], right))
            t = V.op(lambda: ve.bn_aggr(mv[i][:, 0:2], st[i][:]), t)
            t = V.op(lambda: ve.tensor_scalar(mv[i][:, 2:3], mv[i][:, 1:2], 1e-5, None, ALU.add), t)
            t = A.op(lambda: ac.activation(mv[i][:, 2:3], mv[i][:, 2:3], ACT.Sqrt), t)
            t = V.op(lambda: ve.reciprocal(mv[i][:, 3:4], mv[i][:, 2:3]), t)
            ta = V.op(lambda: ve.tensor_scalar(XO[:, 0:HW], left, mv[i][:, 0:1], mv[i][:, 3:4], ALU.subtract, ALU.mult),
                      t, *free["xo_l"])
            tb = V.op(lambda: ve.tensor_scalar(XO[:, HW:D], right, mv[i][:, 0:1], mv[i][:, 3:4], ALU.subtract, ALU.mult))
            return ta, tb
        free["xo_l"] = []

        def transposes(src, parts, dst, t):
            done = []
            for g in range(parts // 4):
                bk = 6 + g
                PE.wait(bank_free[bk], t)
                for j in range(4):
                    tt = PE.op(lambda j=j, g=g, bk=bk: te.transpose(
                        bank[bk][:, j * T:(j + 1) * T], src[:, (4 * g + j) * 128:(4 * g + j + 1) * 128],
                        ident[0:T, 0:T]))
                q, e = (A, ac) if g else (V, ve)
                v = bank[bk][:, 0:4 * T].rearrange("p (a c) -> p a c", c=T)
                cp = (lambda g=g, v=v: ac.copy(XT[:, 4 * g:4 * g + 4, :], v)) if g else \
                    (lambda g=g, v=v: ve.tensor_copy(XT[:, 4 * g:4 * g + 4, :], v))
                ev = q.op(cp, tt, free["xt"])
                bank_free[bk] = ev
                done.append(ev)
            w = s_xt.dma(S, sy, dst, XT[:, 0:parts, :], *done)
            free["xt"] = w
            return tt, w

        def finish_tile(box, d, layer):
            def tail(_):
                ta = box["ln"]
                s1 = s_xo.dma(S, sy, x_d[layer][d], XO[:], *ta)
                extra = []
                if layer == 1:
                    for j, col in ((0, PQ[0][1]), (1, PQ[0][0])):
                        extra.append(V.op(lambda j=j, col=col: ve.tensor_tensor_reduce(
                            out=GS[:], in0=XO[:], in1=GW[0:T, j, :], scale=1.0, scalar=0.0, op0=ALU.mult,
                            op1=ALU.add, accum_out=col[:, d:d + 1]), *ta, tok["wal"], (V.sem, V.n)))
                    tok["pq"] = extra[-1]
                tt, w = transposes(XO, 8, xT_d[layer + 1][d].rearrange("p (k n) -> p k n", k=8), ta[1])
                tok["xd", layer, d] = s1
                tok["xT", layer + 1, d] = w
                free["xo_l"] = [s1, tt] + extra
            return tail

        GS = sb("GS", [T, D], bf)

        def gates(n, src, slot, *waits):
            for j, col in enumerate(PQ[slot]):
                t = V.op(lambda j=j, col=col: ve.tensor_tensor_reduce(
                    out=GS[:, 0:HW], in0=src, in1=GW[0:T, slot, j * HW:(j + 1) * HW], scale=1.0, scalar=0.0,
                    op0=ALU.mult, op1=ALU.add, accum_out=col[:, n:n + 1]), *waits, (V.sem, V.n))
            free["gw"][slot] = t
            tok["pq"] = t
            return t

        def load_gw(k):
            i = k % 2
            tok["gw", k] = s_gw[i].dma(S, sy, GW[:, i, :], gw[k].rearrange("c o -> o c").partition_broadcast(128)
                                       .rearrange("p o c -> p (o c)"), free["gw"][i])

        def add(job):
            jobs.append(job)
            return len(jobs) - 1

        def post_x1(n):
            def post(box):
                b, t = box["b"], box["t"]
                r, tr = box["r"]
                tg = V.op(lambda: ve.tensor_tensor(G[:, n, :], bank[b][0:T, :], B[0:T, :], ALU.add), t, tok["b"])
                bank_free[b] = tg
                free["b"] = tg
                ty = V.op(lambda: ve.tensor_tensor(R[r][:], R[r][:], G[:, n, :], ALU.add), tg, tr)
                w = s_r[r].dma(S, sy, yl_d[n], R[r][:], ty)
                free["r"][r] = w
                tok["yl", n] = w
                gates(n, G[:, n, :], 0, tok["gw", 0], tg)
                split_z(n, G[:, n, :], DIS, tg, tdeg)
            return post

        def prep_x1(n):
            px = prep_x(xT_d[0][n], lambda: ())
            def prep(box):
                if n == 0:
                    load_b(b1)
                    load_gw(0)
                    load_gw(1)
                px(box)
                box["r"] = load_r(x[n * T:(n + 1) * T, 0:HW])
            return prep

        for n in range(NT):
            j = add(Job(mm_x(hW1), prep_x1(n), post_x1(n), w=hW1))

        def bcast_job(col, bias=None):
            def mm(box):
                tpq = tok["pq"]
                box["ev"] = []
                for g, (u, w) in enumerate(((0, 4), (4, 8), (8, 10))):
                    b = take()
                    PE.wait(tpq, bank_free[b])
                    for k in range(u, w):
                        t = PE.op(lambda k=k, u=u, b=b: te.matmul(
                            bank[b][0:T, (k - u) * T:(k - u + 1) * T], col[:, k:k + 1].to_broadcast([T, T]),
                            ident[0:T, 0:T], start=True, stop=True))
                    v = bank[b][0:T, 0:(w - u) * T].rearrange("p (a c) -> p a c", c=T)
                    if bias is None:
                        ev = A.op(lambda u=u, w=w, v=v: ac.copy(PB[:, u:w, :], v), t, free["pb"])
                    else:
                        ev = A.op(lambda u=u, w=w, v=v: ac.activation(PB[:, u:w, :], v, ACT.Identity,
                                                                      bias=bias), t, free["pb"])
                    bank_free[b] = ev
                tok["pb"] = ev
            return mm

        for k in range(4):
            after = len(jobs) - 1
            jb = add(Job(bcast_job(PQ[k % 2][0], GB[0:T, k:k + 1])))
            for d in range(NT):
                def prep(box, d=d, k=k, p=prep_m("gate", d, k % 2)):
                    if k < 2 and d == 5:
                        load_gw(k + 2)
                    p(box)

                def late(box, d=d):
                    box["r1"] = load_r(yl_d[d], tok["yl", d])
                    box["r2"] = load_r(x[d * T:(d + 1) * T, HW:D])

                def post(box, d=d, k=k):
                    b, t = box["b"], box["t"]
                    tg = V.op(lambda: ve.scalar_tensor_tensor(G[:, d, :], bank[b][0:T, :], DIS[:, d:d + 1], G[:, d, :],
                                                             ALU.mult, ALU.add), t, tdeg, *tok["z", d])
                    bank_free[b] = tg
                    if k < 3:
                        gates(d, G[:, d, :], (k + 1) % 2, tok["gw", k + 1], tg, free["pb"])
                        if d == NT - 1:
                            tm = tok["magg"]
                            for n in range(NT):
                                split_z(n, G[:, n, :], DIS, tm, tg)
                    else:
                        (r1, t1), (r2, t2) = box["r1"], box["r2"]
                        tr = V.op(lambda: ve.tensor_tensor(R[r2][:], R[r2][:], G[:, d, :], ALU.add), t2, tg)
                        ln = norm(R[r1][:], R[r2][:], (t1, tr))
                        free["r"][r1] = free["r"][r2] = ln[1]
                        box["ln"] = ln
                box_tail = None
                job = Job(mm_m("gate"), prep, post, after=jb)
                if k == 3:
                    job.late = late
                    job.tail = (lambda box, d=d: finish_tile(box, d, 0)(box))
                last_job = add(job)

        def half_src(layer_T, d):
            return layer_T[d]

        for l in range(2):
            src = xT_d[1] if l == 0 else hT_d
            base = len(jobs)
            kind = "mean"
            bias = b0 if l == 0 else bb1
            prev_last = len(jobs) - NT
            if l == 0:
                prev0 = len(jobs) - NT
                dep = [prev0 + n for n in range(NT)]
            else:
                dep = [prev_agg[n] for n in range(NT)]
            rdy = (lambda n: (tok["xT", 1, n],)) if l == 0 else (lambda n: (tok["hT", 0, n], tok["hT", 1, n]))
            prev_agg = []
            for f in range(2):
                hZ = 1 + 4 * l + 2 * f
                hS = hZ + 1
                for n in range(NT):
                    def postz(box, n=n):
                        tl, th = split_z(n, bank[box["b"]][0:T, :], None, box["t"])
                        bank_free[box["b"]] = tl
                    add(Job(mm_x(hZ), prep_x(src[n], lambda n=n, r=rdy: r(n)), postz, after=dep[n], w=hZ))
                for d in range(NT):
                    boxes = {}

                    def prepa(box, d=d, f=f, l=l, p=prep_m("mean", d), bias=bias):
                        if d == 0:
                            load_b(bias[f * HW:(f + 1) * HW])
                        p(box)

                    def posta(box, d=d, boxes=boxes):
                        b, t = box["b"], box["t"]
                        i = nxt("u", 2)
                        tv = V.op(lambda: ve.scalar_tensor_tensor(U[i][:], bank[b][0:T, :], DEGI[:, d:d + 1], B[0:T, :],
                                                                 ALU.mult, ALU.add), t, tok["b"], free["u"][i])
                        bank_free[b] = tv
                        free["b"] = tv
                        boxes["u"] = (i, tv)
                    add(Job(mm_m(kind), prepa, posta))

                    px = prep_x(src[d], lambda n=d, r=rdy: r(n))
                    if l == 0:
                        def posts(box, d=d, f=f, boxes=boxes):
                            i, tv = boxes["u"]
                            b, t = box["b"], box["t"]
                            t1 = V.op(lambda: ve.tensor_tensor(U[i][:], U[i][:], bank[b][0:T, :], ALU.add), t, tv)
                            bank_free[b] = t1
                            box["h"] = (i, A.op(lambda: ac.activation(U[i][:], U[i][:], ACT.Relu), t1))

                        def tails(box, d=d, f=f):
                            i, t = box["h"]
                            tt, w = transposes(U[i], 4, hT_d[d].rearrange("p (k n) -> p k n", k=8)[:, 4 * f:4 * f + 4, :],
                                               t)
                            tok["hT", f, d] = w
                            free["u"][i] = tt
                        job = Job(mm_x(hS), px, posts, tails, w=hS)
                    else:
                        def preps(box, d=d, f=f, px=px):
                            px(box)
                            box["r"] = load_r(x_d[0][d][:, f * HW:(f + 1) * HW], tok["xd", 0, d])

                        def posts(box, d=d, f=f, boxes=boxes):
                            i, tv = boxes["u"]
                            r, tr = box["r"]
                            b, t = box["b"], box["t"]
                            t1 = V.op(lambda: ve.tensor_tensor(U[i][:], U[i][:], bank[b][0:T, :], ALU.add), t, tv)
                            bank_free[b] = t1
                            if f == 0:
                                t2 = V.op(lambda: ve.tensor_tensor(G[:, d, :], U[i][:], R[r][:], ALU.add), t1, tr)
                                free["u"][i] = free["r"][r] = t2
                            else:
                                t2 = V.op(lambda: ve.tensor_tensor(R[r][:], U[i][:], R[r][:], ALU.add), t1, tr)
                                free["u"][i] = t2
                                box["ln"] = norm(G[:, d, :], R[r][:], (t2,))
                                free["r"][r] = box["ln"][1]
                        job = Job(mm_x(hS), preps, posts, w=hS)
                        if f == 1:
                            job.tail = (lambda box, d=d: finish_tile(box, d, 1)(box))
                    j = add(job)
                    if f == 1:
                        prev_agg.append(j)
                if l == 0 and f == 0:
                    def mmw(box):
                        for j in range(2):
                            for g in range(2):
                                b = take()
                                PE.wait(bank_free[b], tWC)
                                for k in range(4):
                                    t = PE.op(lambda j=j, g=g, k=k, b=b: te.matmul(
                                        bank[b][:, k * 128:(k + 1) * 128],
                                        WC[:, j, 4 * g + k:4 * g + k + 1].to_broadcast([128, 128]), ident[:, :],
                                        start=True, stop=True))
                                ev = A.op(lambda j=j, g=g, b=b: ac.copy(GW[:, j, g * HW:(g + 1) * HW], bank[b][:]), t,
                                          free["gw"][0], free["gw"][1])
                                bank_free[b] = ev
                        tok["wal"] = ev
                    add(Job(mmw))

        base = 9
        dep = prev_agg
        prev_agg = []
        for f in range(2):
            hZ = base + f
            for n in range(NT):
                def postz(box, n=n):
                    tl, th = split_z(n, bank[box["b"]][0:T, :], None, box["t"])
                    bank_free[box["b"]] = tl
                add(Job(mm_x(hZ), prep_x(xT_d[2][n], lambda n=n: (tok["xT", 2, n],)), postz, after=dep[n], w=hZ))
                if f == 0 and n == 3:
                    jb = add(Job(bcast_job(PQ[0][1]), after=dep[-1]))
            for d in range(NT):
                def prep(box, d=d, f=f, p=prep_m("att", d)):
                    p(box)
                    box["r"] = load_r(x_d[1][d][:, f * HW:(f + 1) * HW], tok["xd", 1, d])

                def post(box, d=d, f=f):
                    b, t = box["b"], box["t"]
                    r, tr = box["r"]
                    if f == 0:
                        q = V.op(lambda: ve.tensor_scalar(RS[:, d:d + 1], bank[7][0:T, 0:1], 1e-5, None, ALU.add), t)
                        bank_free[7] = q
                        t = V.op(lambda: ve.reciprocal(RS[:, d:d + 1], RS[:, d:d + 1]), q)
                    i, j = nxt("u", 2), nxt("u", 2)
                    tv = V.op(lambda: ve.tensor_scalar(U[i][:], bank[b][0:T, :], RS[:, d:d + 1], None, ALU.mult), t,
                              free["u"][i])
                    bank_free[b] = tv
                    tm = V.op(lambda: ve.tensor_scalar(U[j][:], U[i][:], 0.0, None, ALU.min), tv, free["u"][j])
                    te_ = A.op(lambda: ac.activation(U[j][:], U[j][:], ACT.Exp), tm)
                    t1 = V.op(lambda: ve.scalar_tensor_tensor(U[i][:], U[i][:], 0.0, U[j][:], ALU.max, ALU.add), te_)
                    free["u"][j] = t1
                    o = G[:, d, :] if f == 0 else R[r][:]
                    t2 = V.op(lambda: ve.scalar_tensor_tensor(o, U[i][:], -1.0, R[r][:], ALU.add, ALU.add), t1, tr)
                    free["u"][i] = t2
                    if f == 0:
                        free["r"][r] = t2
                    else:
                        box["ln"] = norm(G[:, d, :], R[r][:], (t2,))
                        free["r"][r] = box["ln"][1]
                job = Job(mm_m("att", rowsum=(f == 0)), prep, post, after=jb)
                if f == 1:
                    job.tail = (lambda box, d=d: finish_tile(box, d, 2)(box))
                j = add(job)
                if f == 1:
                    prev_agg.append(j)

        dep = prev_agg
        for f in range(2):
            hZ = 11 + f
            for n in range(NT):
                def postz(box, n=n):
                    tl, th = split_z(n, bank[box["b"]][0:T, :], D3, box["t"], tdeg)
                    bank_free[box["b"]] = tl
                add(Job(mm_x(hZ), prep_x(xT_d[3][n], lambda n=n: (tok["xT", 3, n],)), postz, after=dep[n], w=hZ))
            for d in range(NT):
                def prep(box, d=d, f=f, p=prep_m("loop", d)):
                    if d == 0:
                        load_b(b3[f * HW:(f + 1) * HW])
                    p(box)
                    box["r"] = load_r(x_d[2][d][:, f * HW:(f + 1) * HW], tok["xd", 2, d])

                def post(box, d=d, f=f):
                    b, t = box["b"], box["t"]
                    r, tr = box["r"]
                    i = nxt("u", 2)
                    tv = V.op(lambda: ve.scalar_tensor_tensor(U[i][:], bank[b][0:T, :], D3[:, d:d + 1], B[0:T, :],
                                                             ALU.mult, ALU.add), t, tok["b"], free["u"][i])
                    bank_free[b] = tv
                    free["b"] = tv
                    o = G[:, d, :] if f == 0 else R[r][:]
                    t2 = V.op(lambda: ve.scalar_tensor_tensor(o, U[i][:], 0.0, R[r][:], ALU.max, ALU.add), tv, tr)
                    free["u"][i] = t2
                    if f == 0:
                        free["r"][r] = t2
                    else:
                        ln = norm(G[:, d, :], R[r][:], (t2,))
                        free["r"][r] = ln[1]
                        w = s_xo.dma(S, sy, out[d * T:(d + 1) * T, :], XO[:], *ln)
                        free["xo_l"] = [w]
                        tok["out"] = w
                add(Job(mm_m("loop"), prep, post))

        LOOK, LAG = 2, 1
        box = [dict() for _ in jobs]
        last_of = {}
        for j, job in enumerate(jobs):
            if job.w is not None:
                last_of[j] = job.w
        final = {}
        for j, w in last_of.items():
            final[w] = j
        prepped = tailed = 0

        def do_tails(upto):
            nonlocal tailed
            while tailed <= upto:
                if jobs[tailed].tail:
                    jobs[tailed].tail(box[tailed])
                tailed += 1

        def do_preps(upto, must):
            nonlocal prepped
            while prepped <= min(upto, len(jobs) - 1):
                q = jobs[prepped]
                if q.after >= tailed:
                    if prepped > must:
                        return
                    do_tails(q.after)
                if q.prep:
                    q.prep(box[prepped])
                prepped += 1

        for j, job in enumerate(jobs):
            do_preps(j, j)
            job.mm(box[j])
            do_tails(j - LAG)
            do_preps(j + LOOK, j)
            if job.post:
                job.post(box[j])
            if j + 1 < len(jobs) and jobs[j + 1].late:
                jobs[j + 1].late(box[j + 1])
            if job.w is not None and final[job.w] == j:
                may_load(job.w)
        do_tails(len(jobs) - 1)
        S.wait(tok["out"], *[(s.sem, s.n) for s in
                             [s_xo, s_xt, s_at] + s_a + s_r])

        block = ctx.enter_context(nc.Block())
        for q, name in ((PE, "tensor"), (V, "vector"), (A, "scalar"), (P, "gpsimd"), (S, "sync")):
            def body(eng, q=q):
                q.emit(eng)
            {"tensor": block.tensor, "vector": block.vector, "scalar": block.scalar, "gpsimd": block.gpsimd,
             "sync": block.sync}[name](body)


_OUTS = [((N, D), "float32")]


def kernel(**inputs):
    import numpy as _np
    import concourse.bacc as _bacc
    from concourse import mybir as _mybir
    from concourse.bass_utils import run_bass_kernel_spmd as _run

    nc = _bacc.Bacc("TRN2", target_bir_lowering=False, num_devices=1)
    get = {k: _np.asarray(v) for k, v in inputs.items()}
    x = get["x"]
    win = _np.array([[lo * T for lo, hi in windows()], [(hi + 1) * T - 1 for lo, hi in windows()]], _np.float32)
    win = _np.tile(win.reshape(1, 2 * NC), (T, 1))
    arrays = {
        "xT": x.reshape(NT, T, 8, 128).transpose(0, 3, 2, 1).reshape(NT, 128, 8 * T),
        "x": x,
        "es": get["src"].reshape(NC, T).T,
        "ed": get["dst"].reshape(NC, T).T,
        "win": win,
        "W1": get["L0_gnn_W1"], "b1": get["L0_gnn_b1"], "gw": get["L0_gnn_gate_w"], "gb": get["L0_gnn_gate_b"],
        "Ws0": get["L1_gnn_W_self0"], "Wn0": get["L1_gnn_W_neigh0"], "b0": get["L1_gnn_b0"],
        "Ws1": get["L1_gnn_W_self1"], "Wn1": get["L1_gnn_W_neigh1"], "bb1": get["L1_gnn_b1"],
        "W2": get["L2_gnn_W"], "a2": get["L2_gnn_a"], "W3": get["L3_gnn_W"], "b3": get["L3_gnn_b"],
    }
    args, named = [], {}
    for name, a in arrays.items():
        a = _np.ascontiguousarray(a)
        named[f"in_{name}"] = a
        args.append(nc.dram_tensor(f"in_{name}", a.shape, _mybir.dt.from_np(a.dtype), kind="ExternalInput").ap())
    o = nc.dram_tensor("out_0", _OUTS[0][0], _mybir.dt.float32, kind="ExternalOutput").ap()
    gnn_program(nc, *args, o)
    r = _run(nc, [named], core_ids=[0])
    return r.results[0]["out_0"]
```

```python
import numpy as np
import concourse.bass as bass
from concourse import mybir
from contextlib import ExitStack

N, D, E = 1250, 1024, 21250
T = 125
NT = N // T
NC = E // T
HW = 512
PER = NC // NT
MARGIN = 2
NSLOT = 8


def windows():
    out = []
    for c in range(NC):
        lo = max(0, -((PER - 1 + MARGIN - c) // PER))
        hi = min(NT - 1, (c + MARGIN) // PER)
        out.append((lo, hi))
    return out


class Queue:

    def __init__(self, sem):
        self.sem, self.n, self.items = sem, 0, []

    def op(self, fn, *waits):
        self.n += 1
        self.items.append((fn, waits, (self.sem, 1)))
        return (self.sem, self.n)

    def quiet(self, fn, *waits):
        self.items.append((fn, waits, None))

    def wait(self, *waits):
        self.items.append((None, waits, None))

    def emit(self, eng):
        seen = {}
        for fn, waits, inc in self.items:
            for w in waits:
                if w is None:
                    continue
                sem, v = w
                if seen.get(id(sem), 0) < v:
                    eng.wait_ge(sem, v)
                    seen[id(sem)] = v
            if fn is None:
                continue
            ins = fn()
            if inc is not None:
                ins.then_inc(*inc)


class Slot:

    def __init__(self, sem):
        self.sem, self.n = sem, 0

    def dma(self, q, eng, out, in_, *waits):
        self.n += 16
        q.items.append((lambda: eng.dma_start(out, in_), waits, (self.sem, 16)))
        return (self.sem, self.n)


class Job:

    def __init__(self, mm, prep=(None, None, None), post=None, tail=None, after=-1, w=None, late=None):
        self.load, self.first, self.second = prep
        self.mm, self.post, self.tail, self.after, self.w, self.late = mm, post, tail, after, w, late


def gnn_program(nc, xT, x, es, ed, win, W1, b1, gw, gb, Ws0, Wn0, b0, Ws1, Wn1, bb1, W2, a2, W3, b3, out):
    f32, fr, bf, f16 = mybir.dt.float32, mybir.dt.float32r, mybir.dt.bfloat16, mybir.dt.float16
    i16, i32 = mybir.dt.int16, mybir.dt.int32
    ALU, ACT = mybir.AluOpType, mybir.ActivationFunctionType
    AXX = mybir.AxisListType.X
    FMAX = 3.0e38

    def dram(name, shape, dt):
        return nc.dram_tensor(name, shape, dt, kind="Internal").ap()

    a_d = dram("a_d", (NT, T, NT * T), i16)
    at_d = dram("at_d", (NT, T, NT * T), i16)
    x_d = [dram(f"x_d{i}", (NT, T, D), f32) for i in range(3)]
    xT_d = [xT] + [dram(f"xT_d{i}", (NT, 128, 8 * T), f32) for i in range(1, 4)]
    hT_d = dram("hT_d", (NT, 128, 8 * T), f32)
    yl_d = dram("yl_d", (NT, T, HW), f32)

    ctx = ExitStack()
    with ctx:
        def sb(name, shape, dt, c=None):
            return (c or ctx).enter_context(nc.sbuf_tensor(name, shape, dt))

        def sem(name):
            return ctx.enter_context(nc.semaphore(name))

        PE, V, A, P, S = (Queue(sem(f"q_{n}")) for n in ("pe", "dve", "act", "pool", "sync"))
        te, ve, ac, po, sy = nc.tensor, nc.vector, nc.scalar, nc.gpsimd, nc.sync

        wh = [sb(f"wh{i}", [128, HW], fr) for i in range(NSLOT)]
        wl = [sb(f"wl{i}", [128, HW], fr) for i in range(NSLOT)]
        ws = [sb(f"ws{i}", [128, HW], f32) for i in range(2)]
        xs = [sb(f"xs{i}", [128, 8, T], f32) for i in range(2)]
        xh = [sb(f"xh{i}", [128, 8, T], fr) for i in range(2)]
        xl = [sb(f"xl{i}", [128, 8, T], fr) for i in range(2)]
        ident = sb("ident", [128, 128], f32)
        ones = sb("ones", [128, 4], f32)
        onesr = sb("onesr", [128, 2], fr)
        DEG = sb("DEG", [T, NT], f32)
        DIS = sb("DIS", [T, NT], f32)
        DEGI = sb("DEGI", [T, NT], f32)
        D3 = sb("D3", [T, NT], f32)
        sm = sb("sm", [128, 16], f32)
        flags = sb("flags", [1, 2], i32)
        WC = sb("WC", [128, 2, 8], f32)
        WP = sb("WP", [128, 2, 2, 8], f32)
        GB = sb("GB", [128, 4], f32)
        PQ = [[sb(f"P{i}", [T, NT], f32), sb(f"Q{i}", [T, NT], f32)] for i in range(2)]
        RS = sb("RS", [T, NT], f32)
        st = [sb(f"st{i}", [T, 12], f32) for i in range(2)]
        mv = [sb(f"mv{i}", [T, 4], f32) for i in range(2)]
        bank = [ctx.enter_context(nc.psum_tensor(f"bank{i}", [128, HW], f32)) for i in range(8)]
        bank_free = [None] * 8
        idle = list(range(6))

        def take():
            return idle.pop(0)

        def give(b, t):
            bank_free[b] = t
            idle.append(b)

        free = {"gw": [None, None], "ar": [None] * 2, "r": [None] * 4, "u": [None] * 2, "t": [None] * 2,
                "m": [None] * 3, "xo": None, "xt": None, "b": None, "pb": None, "st": [None] * 2}
        cnt = {"ar": 0, "m": 0, "r": 0, "u": 0, "t": 0, "st": 0}
        halves = []
        wsl = [Slot(sem(f"s_ws{i}")) for i in range(6)]
        slot_free = [()] * NSLOT
        w_tok = {}
        nslab = [0]

        def add_half(ap):
            halves.append(ap)
            return len(halves) - 1

        stages = []
        staged = []
        nstaged = [0]

        def stage_slabs(h):
            wide = 2 <= h <= 9
            while nstaged[0] < 8 * min(h + 1, len(halves)):
                pick = [x for x in stages[:6 if wide else 2] if not x["busy"]]
                if not pick:
                    return
                x = min(pick, key=lambda x: x["turn"])
                g = nstaged[0]
                nstaged[0] += 1
                k = g % 8
                waits = [x["free"]] + ([free["t"][x["t"]]] if x["t"] is not None else [])
                t = x["slot"].dma(S, sy, x["ap"], halves[g // 8][k * 128:(k + 1) * 128, :], *waits)
                x["busy"], x["turn"] = True, g
                staged.append((g, x, t))

        def split_slab():
            g, x, t = staged.pop(0)
            s = g % NSLOT
            th = A.op(lambda: ac.copy(wh[s][:], x["ap"]), t, *slot_free[s])
            q, e = (P, po) if g % 2 else (V, ve)
            tl = q.op(lambda: e.tensor_tensor(wl[s][:], x["ap"], wh[s][:].bitcast(f32), ALU.subtract), t, th,
                      *slot_free[s])
            x["free"], x["busy"] = tl, False
            if x["t"] is not None:
                free["t"][x["t"]] = tl
            w_tok[g // 8, g % 8] = (s, th, tl)

        def may_load(done):
            while nslab[0] < 8 * len(halves) and (nslab[0] < NSLOT or (nslab[0] - NSLOT) // 8 <= done):
                if not staged:
                    stage_slabs(nslab[0] // 8)
                split_slab()
                nslab[0] += 1
                stage_slabs((nslab[0] - 1) // 8)

        xsl = [Slot(sem(f"s_xs{i}")) for i in range(2)]
        x_turn = [0]
        xs_free = [(), ()]
        x_free = [None, None]

        def prep_x(src, ready):
            def load(box):
                i = x_turn[0] % 2
                x_turn[0] += 1
                t = xsl[i].dma(S, sy, xs[i][:], src.rearrange("p (k n) -> p k n", k=8), *xs_free[i], *ready())
                box["x"] = (i, t)

            def first(box):
                i, t = box["x"]
                box["x"] = (i, t, A.op(lambda: ac.copy(xh[i][:], xs[i][:]), t, x_free[i]))

            def second(box):
                i, t, th = box["x"]
                tl = V.op(lambda: ve.tensor_tensor(xl[i][:], xs[i][:], xh[i][:].bitcast(f32), ALU.subtract), t, th,
                          x_free[i])
                xs_free[i] = (tl,)
                box["x"] = (i, th, tl)
            return load, first, second

        def mm_x(h):
            def mm(box):
                i, th, tl = box["x"]
                b = take()
                PE.wait(th, tl, bank_free[b])
                for k in range(8):
                    s, wth, wtl = w_tok[h, k]
                    PE.wait(wth, wtl)
                    o = bank[b][0:T, :]
                    PE.quiet(lambda k=k, s=s: te.matmul(o, xh[i][:, k, :], wh[s][:], start=(k == 0), stop=False))
                    PE.quiet(lambda k=k, s=s: te.matmul(o, xh[i][:, k, :], wl[s][:], start=False, stop=False))
                    f = (lambda k=k, s=s: te.matmul(o, xl[i][:, k, :], wh[s][:], start=False, stop=(k == 7)))
                    if k < 7:
                        PE.quiet(f)
                t = PE.op(f)
                x_free[i] = t
                for k in range(8):
                    slot_free[w_tok[h, k][0]] = (t,)
                box["b"], box["t"] = b, t
            return mm

        hW1 = add_half(W1)
        for wn, wsf in ((Wn0, Ws0), (Wn1, Ws1)):
            for f in range(2):
                add_half(wn[:, f * HW:(f + 1) * HW])
                add_half(wsf[:, f * HW:(f + 1) * HW])
        for w in (W2, W3):
            for f in range(2):
                add_half(w[:, f * HW:(f + 1) * HW])

        WIN = windows()
        c_first = {b: min(c for c in range(NC) if WIN[c][0] <= b <= WIN[c][1]) for b in range(NT)}
        c_last = {b: max(c for c in range(NC) if WIN[c][0] <= b <= WIN[c][1]) for b in range(NT)}
        PC = [(0, 417), (417, 834), (834, 1250)]

        Zh = sb("Zh", [T, NT, HW], fr)
        Zl = sb("Zl", [T, NT, HW], fr)
        G = sb("G", [T, NT, HW], f32)
        GW = sb("GW", [128, 2, D], f32)
        B = sb("B", [128, HW], f32)
        GSF = sb("GSF", [128, D], bf)
        GS, GS2 = GSF[0:T, :], GSF[:, 0:HW]

        ca = ExitStack()
        ei = sb("ei", [T, 2, NC], i32, ca)
        ef = sb("ef", [T, 2, NC], f32, ca)
        wn_ = sb("wn_", [T, 2, NC], f32, ca)
        wt = sb("wt", [T, 2, NC], f32, ca)
        iot = sb("iot", [T, N], f16, ca)
        oS = [sb(f"oS{i}", [T, N], bf, ca) for i in range(4)]
        oD = [sb(f"oD{i}", [T, 2 * T], bf, ca) for i in range(4)]
        zz = sb("zz", [T, HW], bf, ca)
        AT = sb("AT", [T, NT, N], i16, ca)
        Af = [sb(f"Af{i}", [T, N], f32, ca) for i in range(2)]
        A16 = [sb(f"A16{i}", [T, NT, T], i16, ca) for i in range(2)]
        ca.close()

        Mh = [sb(f"Mh{i}", [T, NT, T], fr) for i in range(3)]
        Ml = [sb(f"Ml{i}", [T, NT, T], fr) for i in range(3)]
        TF = [sb(f"Tt{i}", [128, NT * T], f32) for i in range(2)]
        Tt = [t[0:T, :].rearrange("p (a c) -> p a c", c=T) for t in TF]
        Ar = [sb(f"Ar{i}", [T, NT, T], i16) for i in range(2)]
        PB = sb("PB", [T, NT, T], f32)
        RF = [sb(f"R{i}", [128, HW], f32) for i in range(4)]
        UF = [sb(f"U{i}", [128, HW], f32) for i in range(2)]
        R, U = [r[0:T, :] for r in RF], [u[0:T, :] for u in UF]
        XO = [sb(f"XO{i}", [T, D], f32) for i in range(2)]
        XT = sb("XT", [128, 8, T], f32)


        s_e, s_c = Slot(sem("s_e")), Slot(sem("s_c"))
        te_ = s_e.dma(S, sy, ei[:, 0, :], es)
        te_ = s_e.dma(S, sy, ei[:, 1, :], ed)
        te_ = s_e.dma(S, sy, wn_[:], win.rearrange("p (a c) -> p a c", a=2))
        tc_ = s_c.dma(S, sy, GB[:], gb.rearrange("k o -> o k").partition_broadcast(128).rearrange("p o k -> p (o k)"))

        ti = P.op(lambda: po.iota(iot[:], [[1, N]], base=0, channel_multiplier=0, allow_small_or_imprecise_dtypes=True))
        t0 = P.op(lambda: po.memset(ident[:], 0.0))
        tid = P.op(lambda: po.affine_select(out=ident[:], in_=ident[:], compare_op=ALU.not_equal, fill=1.0, base=0,
                                            pattern=[[-1, 128]], channel_multiplier=1), t0)
        to = P.op(lambda: po.memset(ones[:], 1.0))
        tz = P.op(lambda: po.memset(zz[:], 0.0))
        tor = V.op(lambda: ve.tensor_copy(onesr[:], ones[:, 0:2]), to)

        t1 = V.op(lambda: ve.tensor_copy(ef[:], ei[:]), te_)
        t2 = V.op(lambda: ve.tensor_tensor(wt[:, 0, :], wn_[:, 0, :], ef[:, 1, :], ALU.subtract), t1)
        t3 = V.op(lambda: ve.tensor_tensor(wt[:, 1, :], ef[:, 1, :], wn_[:, 1, :], ALU.subtract), t1)
        t4 = V.op(lambda: ve.reduce_max(sm[0:T, 0:1], wt[:].rearrange("p a c -> p (a c)"), AXX), t2, t3)
        t5 = V.op(lambda: ve.tensor_scalar(sm[0:T, 1:2], sm[0:T, 0:1], 0.0, None, ALU.is_gt), t4)
        t6 = PE.op(lambda: te.matmul(bank[7][0:1, 0:1], sm[0:T, 1:2], ones[0:T, 0:1], start=True, stop=True), t5, to)
        tflag = V.op(lambda: ve.tensor_copy(flags[0:1, 0:1], bank[7][0:1, 0:1]), t6)

        for i in range(6):
            stages.append({"slot": wsl[i], "ap": ws[i][:] if i < 2 else TF[i // 2 - 1][:, (i % 2) * HW:(i % 2) * HW + HW],
                           "t": None if i < 2 else i // 2 - 1, "free": None, "busy": False, "turn": -1})
        may_load(-1)

        fS, fP, fE = sem("fS"), sem("fP"), sem("fE")
        gS, gP, gB, gE = sem("gS"), sem("gP"), sem("gB"), sem("gE")
        eng_of = {id(PE): te, id(V): ve, id(A): ac}

        def one_hots(c, i, col):
            ve.tensor_scalar(oS[i][:], iot[:], ef[:, 0, col], None, ALU.is_equal).then_inc(*c)

        def dve_build():
            v = ve.value_load(flags[0:1, 0:1], min_val=0, max_val=T)
            with ve.If(v < 1):
                for c in range(NC):
                    i = c % 4
                    lo, hi = WIN[c]
                    if c >= 4:
                        ve.wait_ge(fP, c - 3)
                    ve.tensor_scalar(oS[i][:], iot[:], ef[:, 0, c:c + 1], None, ALU.is_equal).then_inc(fS, 1)
                    n = (hi - lo + 1) * T
                    ve.tensor_scalar(oD[i][:, 0:n], iot[:, lo * T:lo * T + n], ef[:, 1, c:c + 1], None,
                                     ALU.is_equal).then_inc(fS, 1)
            with ve.Else():
                for b in range(NT):
                    with ve.Fori(0, NC) as c:
                        ve.wait_ge(gP, 1)
                        ve.sem_clear(gP)
                        ve.tensor_scalar(oS[0][:], iot[:], ef[:, 0, bass.ds(c, 1)], None, ALU.is_equal).then_inc(gS, 1)
                        ve.tensor_scalar(oD[0][:, 0:T], iot[:, b * T:(b + 1) * T], ef[:, 1, bass.ds(c, 1)], None,
                                         ALU.is_equal).then_inc(gS, 1)

        def pe_build():
            v = te.value_load(flags[0:1, 0:1], min_val=0, max_val=T)
            with te.If(v < 1):
                for c in range(NC):
                    i = c % 4
                    lo, hi = WIN[c]
                    te.wait_ge(fS, 2 * (c + 1))
                    for b in range(lo, hi + 1):
                        if c == c_first[b] and b >= 2:
                            te.wait_ge(fE, b - 1)
                        for j, (u, w) in enumerate(PC):
                            m = te.matmul(bank[3 * (b % 2) + j][0:T, 0:w - u], oD[i][:, (b - lo) * T:(b - lo + 1) * T],
                                          oS[i][:, u:w], start=(c == c_first[b]), stop=(c == c_last[b]))
                    m.then_inc(fP, 1)
            with te.Else():
                te.sem_inc(gP, 1)
                for b in range(NT):
                    if b:
                        te.wait_ge(gE, b)
                    for j, (u, w) in enumerate(PC):
                        te.matmul(bank[j][0:T, 0:w - u], zz[:, 0:T], zz[:, 0:w - u], start=True, stop=False)
                    with te.Fori(0, NC) as c:
                        te.wait_ge(gS, 2)
                        te.sem_clear(gS)
                        for j, (u, w) in enumerate(PC):
                            m = te.matmul(bank[j][0:T, 0:w - u], oD[0][:, 0:T], oS[0][:, u:w], start=False, stop=False)
                        m.then_inc(gP, 1)
                    for j, (u, w) in enumerate(PC):
                        m = te.matmul(bank[j][0:T, 0:w - u], zz[:, 0:T], zz[:, 0:w - u], start=False, stop=True)
                    m.then_inc(gB, 1)

        def act_build():
            v = ac.value_load(flags[0:1, 0:1], min_val=0, max_val=T)
            with ac.If(v < 1):
                for b in range(NT):
                    ac.wait_ge(fP, c_last[b] + 1)
                    for j, (u, w) in enumerate(PC):
                        m = ac.copy(AT[:, b, u:w], bank[3 * (b % 2) + j][0:T, 0:w - u])
                    m.then_inc(fE, 1)
            with ac.Else():
                for b in range(NT):
                    ac.wait_ge(gB, b + 1)
                    for j, (u, w) in enumerate(PC):
                        m = ac.copy(AT[:, b, u:w], bank[j][0:T, 0:w - u])
                    m.then_inc(gE, 1)

        V.wait(t1, ti, tflag)
        V.quiet(lambda: (dve_build(), None)[1])
        PE.wait(tz, tflag)
        PE.quiet(lambda: (pe_build(), None)[1])
        A.wait(tflag)
        A.quiet(lambda: (act_build(), None)[1])
        tA = A.op(lambda: ac.copy(sm[0:1, 8:9], ident[0:1, 0:1]), tid)
        tPE = PE.op(lambda: te.matmul(bank[7][0:1, 0:1], ones[0:1, 0:1], ones[0:1, 0:1], start=True, stop=True), tflag)
        for b in range(8):
            bank_free[b] = tA

        s_at = Slot(sem("s_at"))
        s_a = [Slot(sem(f"s_a{i}")) for i in range(2)]
        af_free = [None, None]
        a16_free = [None, None]
        af_tok = [None] * NT
        big = {}

        def counts_float(b):
            i = b % 2
            tf = V.op(lambda: ve.tensor_copy(Af[i][:], AT[:, b, :]), tA, af_free[i])
            af_tok[b] = tf
            V.op(lambda: ve.reduce_sum(DEG[:, b:b + 1], Af[i][:], AXX), tf)

        def counts_out(b):
            i = b % 2
            s_at.dma(S, sy, at_d[:, :, b * T:(b + 1) * T].rearrange("t p s -> p t s"),
                     AT[:, b, :].rearrange("p (t s) -> p t s", t=NT), tA)
            for u, w in ((0, 4), (4, 8), (8, 10)):
                bk = take()
                PE.wait(af_tok[b], bank_free[bk], tid)
                for j in range(u, w):
                    fn = (lambda j=j, u=u, bk=bk: te.transpose(bank[bk][0:T, (j - u) * T:(j - u + 1) * T],
                                                              Af[i][:, j * T:(j + 1) * T], ident[0:T, 0:T]))
                    tt = PE.op(fn)
                ev = A.op(lambda u=u, w=w, bk=bk: ac.copy(
                    A16[i][:, u:w, :], bank[bk][0:T, 0:(w - u) * T].rearrange("p (a c) -> p a c", c=T)), tt, a16_free[i])
                give(bk, ev)
            af_free[i] = (V.sem, V.n) if False else tt
            a16_free[i] = s_a[i].dma(S, sy, a_d[b].rearrange("p (a c) -> p a c", c=T), A16[i][:], ev)

        def leave_build(_):
            dd = (V.sem, V.n)
            t = V.op(lambda: ve.tensor_scalar(DEGI[:], DEG[:], 1.0, None, ALU.max), dd)
            t = V.op(lambda: ve.reciprocal(DEGI[:], DEGI[:]), t)
            t = V.op(lambda: ve.tensor_scalar(D3[:], DEG[:], 1.0, None, ALU.add), t)
            t = V.op(lambda: ve.reciprocal(D3[:], D3[:]), t)
            A.op(lambda: ac.activation(DIS[:], DEGI[:], ACT.Sqrt), t)
            tok["deg"] = A.op(lambda: ac.activation(D3[:], D3[:], ACT.Sqrt), t)
            t = V.op(lambda: ve.reduce_max(sm[0:T, 2:3], DEG[:], AXX), dd)
            t = V.op(lambda: ve.tensor_scalar(sm[0:T, 3:4], sm[0:T, 2:3], 4096.0, None, ALU.is_gt), t)
            t = PE.op(lambda: te.matmul(bank[7][0:1, 0:1], sm[0:T, 3:4], ones[0:T, 0:1], start=True, stop=True), t)
            t = V.op(lambda: ve.tensor_copy(flags[0:1, 1:2], bank[7][0:1, 0:1]), t)
            bank_free[7] = t
            PE.quiet(lambda: big.update(v=te.value_load(flags[0:1, 1:2], min_val=0, max_val=T)), t)
            ends = [(PE.sem, PE.n), (V.sem, V.n), (A.sem, A.n), (P.sem, P.n), (s_at.sem, s_at.n),
                    a16_free[0], a16_free[1]]
            for q in (PE, V, A, P, S):
                q.wait(*ends)


        jobs = []
        s_gw = [Slot(sem(f"s_gw{i}")) for i in range(2)]
        s_ar = [Slot(sem(f"s_ar{i}")) for i in range(2)]
        s_r = [Slot(sem(f"s_r{i}")) for i in range(4)]
        s_b = Slot(sem("s_b"))
        s_xo, s_xt, s_u = [Slot(sem(f"s_xo{i}")) for i in range(2)], Slot(sem("s_xt")), [Slot(sem(f"s_u{i}")) for i in range(2)]
        tok = {}

        def nxt(name, n):
            i = cnt[name] % n
            cnt[name] += 1
            return i

        def load_r(src, *waits):
            i = nxt("r", 4)
            return i, s_r[i].dma(S, sy, R[i][:], src, free["r"][i], *waits)

        def load_b(src):
            tok["b"] = s_b.dma(S, sy, B[:], src.rearrange("(o c) -> o c", o=1).partition_broadcast(128).rearrange("p o c -> p (o c)"), free["b"])

        def prep_m(kind, d, par=0):
            def load(box):
                r = nxt("ar", 2)
                src = at_d if kind == "att" else a_d
                ta = s_ar[r].dma(S, sy, Ar[r][:], src[d].rearrange("p (a c) -> p a c", c=T), free["ar"][r])
                if kind in ("gate", "att"):
                    i = nxt("t", 2)
                    col = PQ[par][1] if kind == "gate" else PQ[0][0]
                    row = PB[:, d, :].unsqueeze(1).to_broadcast([T, NT, T])
                    cb = col[:].unsqueeze(2).to_broadcast([T, NT, T])
                    t = P.op(lambda: po.tensor_tensor(Tt[i][:], row, cb, ALU.add), free["t"][i], tok["pb"], tok["pq"])
                    free["pb"] = t
                    if kind == "gate":
                        t = A.op(lambda: ac.activation(Tt[i][:], Tt[i][:], ACT.Tanh), t)
                        t = V.op(lambda: ve.tensor_tensor(Tt[i][:], Tt[i][:], Ar[r][:], ALU.mult), t, ta)
                    else:
                        t = V.op(lambda: ve.scalar_tensor_tensor(Tt[i][:], Tt[i][:], 0.1, Tt[i][:], ALU.mult, ALU.max),
                                 t)
                        t = A.op(lambda: ac.activation(Tt[i][:], Tt[i][:], ACT.Exp, scale=-1.0), t)
                        t = V.op(lambda: ve.scalar_tensor_tensor(Tt[i][:], Tt[i][:], FMAX, Ar[r][:], ALU.min, ALU.mult),
                                 t, ta)
                    free["ar"][r] = t
                    box["in"] = (Tt[i], t, "t", i)
                else:
                    if kind == "loop":
                        ta = V.op(lambda: ve.tensor_tensor(Ar[r][:, d, :], Ar[r][:, d, :], ident[0:T, 0:T], ALU.add), ta)
                    box["in"] = (Ar[r], ta, "ar", r)

            def first(box):
                M, t, _, _ = box["in"]
                i = nxt("m", 3)
                box["m"] = (i, A.op(lambda: ac.copy(Mh[i][:], M[:]), t, free["m"][i]))

            def second(box):
                M, t, name, k = box["in"]
                i, th = box["m"]
                tl = V.op(lambda: ve.tensor_tensor(Ml[i][:], M[:], Mh[i][:].bitcast(f32), ALU.subtract), th, t,
                          free["m"][i])
                free[name][k] = tl
                box["m"] = (i, th, tl)
            return load, first, second

        def mm_m(kind, rowsum=False):
            def mm(box):
                i, th, tl = box["m"]
                b = take()
                o = bank[b][0:T, :]
                PE.wait(bank_free[b], th)
                full = kind in ("gate", "att")
                for s in range(NT):
                    PE.wait(*tok["z", s])
                    PE.quiet(lambda s=s: te.matmul(o, Mh[i][:, s, :], Zh[:, s, :], start=(s == 0), stop=False))
                    if full:
                        PE.quiet(lambda s=s: te.matmul(o, Mh[i][:, s, :], Zl[:, s, :], start=False, stop=False))
                        PE.wait(tl)
                        f = (lambda s=s: te.matmul(o, Ml[i][:, s, :], Zh[:, s, :], start=False, stop=(s == NT - 1)))
                    else:
                        f = (lambda s=s: te.matmul(o, Mh[i][:, s, :], Zl[:, s, :], start=False, stop=(s == NT - 1)))
                        if s == 0:
                            def extra():
                                with te.If(big["v"] > 0):
                                    for r in range(NT):
                                        te.matmul(o, Ml[i][:, r, :], Zh[:, r, :], start=False, stop=False)
                            zt = [tok["z", r] for r in range(NT)]
                            box["extra"] = (extra, zt)
                    if s < NT - 1:
                        PE.quiet(f)
                if "extra" in box:
                    PE.quiet(box["extra"][0], tl, *[w for z in box["extra"][1] for w in z])
                t = PE.op(f)
                if rowsum:
                    rb = 7
                    for s in range(NT):
                        for m, (M, z) in enumerate(((Mh, 0), (Ml, 1))):
                            f2 = (lambda s=s, M=M, z=z: te.matmul(bank[rb][0:T, 0:2], M[i][:, s, :], onesr[0:T, :],
                                                                  start=(s == 0 and z == 0),
                                                                  stop=(s == NT - 1 and z == 1)))
                            if s == 0 and m == 0:
                                PE.wait(bank_free[rb], tor)
                            if not (s == NT - 1 and m == 1):
                                PE.quiet(f2)
                    t = PE.op(f2)
                free["m"][i] = t
                tok["magg"] = t
                box["b"], box["t"] = b, t
            return mm

        def split_z(n, src, scale, *waits):
            sc = None if scale is None else scale[:, n:n + 1]
            if sc is None:
                th = A.op(lambda: ac.copy(Zh[:, n, :], src), *waits)
                tl = V.op(lambda: ve.tensor_tensor(Zl[:, n, :], src, Zh[:, n, :].bitcast(f32), ALU.subtract), th, *waits)
            else:
                th = A.op(lambda: ac.activation(Zh[:, n, :], src, ACT.Copy, scale=sc), *waits)
                tl = V.op(lambda: ve.scalar_tensor_tensor(Zl[:, n, :], src, sc, Zh[:, n, :].bitcast(f32), ALU.mult,
                                                         ALU.subtract), th, *waits)
            tok["z", n] = (th, tl)
            return tl, th

        def norm(left, right, waits):
            i = nxt("st", 2)
            X = XO[i]
            V.op(lambda: ve.bn_stats(st[i][:, 0:6], left), *waits)
            t = V.op(lambda: ve.bn_stats(st[i][:, 6:12], right))
            t = V.op(lambda: ve.bn_aggr(mv[i][:, 0:2], st[i][:]), t)
            t = V.op(lambda: ve.tensor_scalar(mv[i][:, 2:3], mv[i][:, 1:2], 1e-5, None, ALU.add), t)
            t = A.op(lambda: ac.activation(mv[i][:, 2:3], mv[i][:, 2:3], ACT.Sqrt), t)
            t = V.op(lambda: ve.reciprocal(mv[i][:, 3:4], mv[i][:, 2:3]), t)
            ta = V.op(lambda: ve.tensor_scalar(X[:, 0:HW], left, mv[i][:, 0:1], mv[i][:, 3:4], ALU.subtract, ALU.mult),
                      t, *free["xo"][i])
            tb = V.op(lambda: ve.tensor_scalar(X[:, HW:D], right, mv[i][:, 0:1], mv[i][:, 3:4], ALU.subtract, ALU.mult))
            return ta, tb, i
        free["xo"] = [[], []]

        def transposes(src, parts, dst, t):
            done = []
            for g in range(parts // 4):
                bk = 6 + g
                PE.wait(bank_free[bk], t)
                for j in range(4):
                    tt = PE.op(lambda j=j, g=g, bk=bk: te.transpose(
                        bank[bk][:, j * T:(j + 1) * T], src[:, (4 * g + j) * 128:(4 * g + j + 1) * 128],
                        ident[0:T, 0:T]))
                q, e = (A, ac) if g else (V, ve)
                v = bank[bk][:, 0:4 * T].rearrange("p (a c) -> p a c", c=T)
                cp = (lambda g=g, v=v: ac.copy(XT[:, 4 * g:4 * g + 4, :], v)) if g else \
                    (lambda g=g, v=v: ve.tensor_copy(XT[:, 4 * g:4 * g + 4, :], v))
                ev = q.op(cp, tt, free["xt"])
                bank_free[bk] = ev
                done.append(ev)
            w = s_xt.dma(S, sy, dst, XT[:, 0:parts, :], *done)
            free["xt"] = w
            return tt, w

        def finish_tile(box, d, layer):
            def tail(_):
                *ta, i = box["ln"]
                X = XO[i]
                s1 = s_xo[i].dma(S, sy, x_d[layer][d], X[:], *ta)
                extra = []
                if layer == 1:
                    for j, col in ((0, PQ[0][1]), (1, PQ[0][0])):
                        extra.append(V.op(lambda j=j, col=col: ve.tensor_tensor_reduce(
                            out=GS[:], in0=X[:], in1=GW[0:T, j, :], scale=1.0, scalar=0.0, op0=ALU.mult,
                            op1=ALU.add, accum_out=col[:, d:d + 1]), *ta, tok["wal"], (V.sem, V.n)))
                    tok["pq"] = extra[-1]
                tt, w = transposes(X, 8, xT_d[layer + 1][d].rearrange("p (k n) -> p k n", k=8), ta[1])
                tok["xd", layer, d] = s1
                tok["xT", layer + 1, d] = w
                free["xo"][i] = [s1, tt] + extra
            return tail

        def gates(n, src, slot, *waits):
            for j, col in enumerate(PQ[slot]):
                t = V.op(lambda j=j, col=col: ve.tensor_tensor_reduce(
                    out=GS[:, 0:HW], in0=src, in1=GW[0:T, slot, j * HW:(j + 1) * HW], scale=1.0, scalar=0.0,
                    op0=ALU.mult, op1=ALU.add, accum_out=col[:, n:n + 1]), *waits, (V.sem, V.n))
            free["gw"][slot] = t
            tok["pq"] = t
            return t

        def load_gw(k):
            i = k % 2
            tok["gw", k] = s_gw[i].dma(S, sy, GW[:, i, :], gw[k].rearrange("c o -> o c").partition_broadcast(128)
                                       .rearrange("p o c -> p (o c)"), free["gw"][i])

        def add(job):
            jobs.append(job)
            return len(jobs) - 1

        s_g = [Slot(sem(f"s_g{i}")) for i in range(2)]

        def post_x1(n):
            def post(box):
                b, t = box["b"], box["t"]
                tg = V.op(lambda: ve.tensor_tensor(G[:, n, :], bank[b][0:T, :], B[0:T, :], ALU.add), t, tok["b"])
                give(b, tg)
                free["b"] = tg
                tok["yl", n] = s_g[n % 2].dma(S, sy, yl_d[n], G[:, n, :], tg, (s_g[n % 2].sem, s_g[n % 2].n))
                gates(n, G[:, n, :], 0, tok["gw", 0], tg)
                counts_out(n)
            return post

        def prep_x1(n):
            load, first, second = prep_x(xT_d[0][n], lambda: ())

            def load_first(box):
                load_b(b1)
                load_gw(0)
                load_gw(1)
                load(box)
            return (load if n else load_first), first, second

        counts_float(0)
        for n in range(NT):
            late = (lambda box, n=n: counts_float(n)) if n else None
            add(Job(mm_x(hW1), prep_x1(n), post_x1(n), w=hW1, late=late))
        add(Job(leave_build, after=len(jobs) - 1))

        def scale_z(ns, *waits):
            for n in ns:
                split_z(n, G[:, n, :], DIS, tok["deg"], *waits)

        s_w2 = [Slot(sem(f"s_w2{i}")) for i in range(2)]
        w2 = {"g": 0}

        def w2_step():
            g = w2["g"]
            if g == 16:
                return
            w2["g"] += 1
            h, k = divmod(g, 8)
            if k == 0:
                w2["a"] = [s_w2[j].dma(S, sy, UF[j][:], a2[0:1, j * D + h * HW:j * D + (h + 1) * HW]
                                       .partition_broadcast(128).rearrange("p o c -> p (o c)"), free["u"][j])
                           for j in range(2)]
            r = nxt("r", 4)
            t = s_r[r].dma(S, sy, RF[r][:], W2[k * 128:(k + 1) * 128, h * HW:(h + 1) * HW], free["r"][r])
            for j in range(2):
                t2 = V.op(lambda j=j: ve.tensor_tensor_reduce(
                    out=GS2[:], in0=RF[r][:], in1=UF[j][:], scale=1.0, scalar=0.0,
                    op0=ALU.mult, op1=ALU.add, accum_out=WP[:, h, j, k:k + 1]), t, w2["a"][j], (V.sem, V.n))
            free["r"][r] = free["u"][0] = free["u"][1] = t2
            if g == 15:
                tok["wc"] = V.op(lambda: ve.tensor_tensor(WC[:], WP[:, 0, :, :], WP[:, 1, :, :], ALU.add), t2)

        def bcast_job(col, bias=None):
            def mm(box):
                tpq = tok["pq"]
                box["ev"] = []
                for g, (u, w) in enumerate(((0, 4), (4, 8), (8, 10))):
                    b = take()
                    PE.wait(tpq, bank_free[b])
                    for k in range(u, w):
                        t = PE.op(lambda k=k, u=u, b=b: te.matmul(
                            bank[b][0:T, (k - u) * T:(k - u + 1) * T], col[:, k:k + 1].to_broadcast([T, T]),
                            ident[0:T, 0:T], start=True, stop=True))
                    v = bank[b][0:T, 0:(w - u) * T].rearrange("p (a c) -> p a c", c=T)
                    if bias is None:
                        ev = A.op(lambda u=u, w=w, v=v: ac.copy(PB[:, u:w, :], v), t, free["pb"])
                    else:
                        ev = A.op(lambda u=u, w=w, v=v: ac.activation(PB[:, u:w, :], v, ACT.Identity,
                                                                      bias=bias), t, free["pb"])
                    give(b, ev)
                tok["pb"] = ev
            return mm

        for k in range(4):
            jb = add(Job(bcast_job(PQ[k % 2][0], GB[0:T, k:k + 1]), after=len(jobs) - 1))
            for d in range(NT):
                load, first, second = prep_m("gate", d, k % 2)

                def load_zs(box, k=k, load=load):
                    waits = () if k == 0 else (tok["magg"], tok["g"])
                    scale_z(range(0, 4), *waits)
                    load(box)
                    scale_z(range(4, NT), *waits)
                    tok["zs"] = True

                def load_w(box, k=k, load=load):
                    load_gw(k + 2)
                    load(box)

                def late(box, d=d):
                    box["r"] = [load_r(yl_d[d], tok["yl", d]), load_r(x[d * T:(d + 1) * T, 0:HW]),
                                load_r(x[d * T:(d + 1) * T, HW:D])]

                def post(box, d=d, k=k):
                    b, t = box["b"], box["t"]
                    tg = V.op(lambda: ve.scalar_tensor_tensor(G[:, d, :], bank[b][0:T, :], DIS[:, d:d + 1], G[:, d, :],
                                                             ALU.mult, ALU.add), t, tok["deg"], *tok["z", d])
                    tok["g"] = tg
                    give(b, tg)
                    if k < 3:
                        gates(d, G[:, d, :], (k + 1) % 2, tok["gw", k + 1], tg, free["pb"])
                        if d % 2 == 0 or k == 0:
                            w2_step()
                    else:
                        (r0, t0), (r1, t1), (r2, t2) = box["r"]
                        tl = V.op(lambda: ve.tensor_tensor(R[r1][:], R[r1][:], R[r0][:], ALU.add), t1, t0)
                        tr = V.op(lambda: ve.tensor_tensor(R[r2][:], R[r2][:], G[:, d, :], ALU.add), t2, tg)
                        ln = norm(R[r1][:], R[r2][:], (tl, tr))
                        free["r"][r0] = tl
                        free["r"][r1] = free["r"][r2] = ln[1]
                        box["ln"] = ln
                prep = (load_zs if d == 0 else load_w if d == 5 and k < 2 else load, first, second)
                job = Job(mm_m("gate"), prep, post, after=jb)
                if k == 3:
                    job.late = late
                    job.tail = (lambda box, d=d: finish_tile(box, d, 0)(box))
                add(job)

        pr2 = [dict() for _ in range(NT)]
        order = [("a", 0), ("a", 1), ("s", 0), ("s", 1), ("s", 2), ("s", 3)]
        for n in range(2, 8):
            order += [("a", n), ("s", n + 2)]
        order += [("a", 8), ("a", 9)]
        dep = [len(jobs) - NT + n for n in range(NT)]
        for l in range(2):
            src = xT_d[1] if l == 0 else hT_d
            bias = b0 if l == 0 else bb1
            if l == 0:
                rdy = lambda n: (tok["xT", 1, n],)
            else:
                rdy = lambda n: (tok["hT", 0, n], tok["hT", 1, n])
            done = {}
            for f in range(2):
                hZ = 1 + 4 * l + 2 * f
                hS = hZ + 1
                for n in range(NT):
                    def postz(box, n=n):
                        tl, th = split_z(n, bank[box["b"]][0:T, :], None, box["t"])
                        give(box["b"], tl)
                    add(Job(mm_x(hZ), prep_x(src[n], lambda n=n, r=rdy: r(n)), postz, after=dep[n], w=hZ))
                pair = [dict() for _ in range(NT)]
                for what, d in order:
                    def post(box, what=what, d=d, f=f, l=l, pair=pair):
                        pr = pair[d]
                        pr[what] = (box["b"], box["t"])
                        if len(pr) < 2:
                            return
                        (b, t), (b2, t2) = pr["a"], pr["s"]
                        i = nxt("u", 2)
                        tv = V.op(lambda: ve.scalar_tensor_tensor(U[i][:], bank[b][0:T, :], DEGI[:, d:d + 1], B[0:T, :],
                                                                 ALU.mult, ALU.add), t, tok["b"], free["u"][i])
                        give(b, tv)
                        free["b"] = tv
                        t1 = V.op(lambda: ve.tensor_tensor(U[i][:], U[i][:], bank[b2][0:T, :], ALU.add), t2, tv)
                        give(b2, t1)
                        if l == 0:
                            box["h"] = (i, A.op(lambda: ac.activation(U[i][:], U[i][:], ACT.Relu), t1))
                            return
                        r, tr = load_r(x_d[0][d][:, f * HW:(f + 1) * HW], tok["xd", 0, d]) if "r" not in pr2[d] \
                            else pr2[d].pop("r")
                        if f == 0:
                            t2 = V.op(lambda: ve.tensor_tensor(G[:, d, :], U[i][:], R[r][:], ALU.add), t1, tr)
                            free["u"][i] = free["r"][r] = t2
                        else:
                            t2 = V.op(lambda: ve.tensor_tensor(R[r][:], U[i][:], R[r][:], ALU.add), t1, tr)
                            free["u"][i] = t2
                            box["ln"] = norm(G[:, d, :], R[r][:], (t2,))
                            free["r"][r] = box["ln"][1]

                    second_one = (what == "a") == (d > 1)
                    if what == "a":
                        load, first, second = prep_m("mean", d)
                        if d == 0:
                            def load(box, load=load, bias=bias, f=f):
                                load_b(bias[f * HW:(f + 1) * HW])
                                load(box)
                        job = Job(mm_m("mean"), (load, first, second), post)
                    else:
                        job = Job(mm_x(hS), prep_x(src[d], lambda n=d, r=rdy: r(n)), post, w=hS)
                    if second_one:
                        if l == 0:
                            def tails(box, d=d, f=f):
                                i, t = box["h"]
                                tt, w = transposes(U[i], 4, hT_d[d].rearrange("p (k n) -> p k n", k=8)
                                                   [:, 4 * f:4 * f + 4, :], t)
                                tok["hT", f, d] = w
                                free["u"][i] = tt
                            job.tail = tails
                        else:
                            def late(box, d=d, f=f):
                                pr2[d]["r"] = load_r(x_d[0][d][:, f * HW:(f + 1) * HW], tok["xd", 0, d])
                            job.late = late
                            if f == 1:
                                job.tail = (lambda box, d=d: finish_tile(box, d, 1)(box))
                    j = add(job)
                    if second_one:
                        done[d] = j
                if l == 0 and f == 0:
                    def mmw(box):
                        for j in range(2):
                            for g in range(2):
                                b = take()
                                PE.wait(bank_free[b], tok["wc"])
                                for k in range(4):
                                    t = PE.op(lambda j=j, g=g, k=k, b=b: te.matmul(
                                        bank[b][:, k * 128:(k + 1) * 128],
                                        WC[:, j, 4 * g + k:4 * g + k + 1].to_broadcast([128, 128]), ident[:, :],
                                        start=True, stop=True))
                                ev = A.op(lambda j=j, g=g, b=b: ac.copy(GW[:, j, g * HW:(g + 1) * HW], bank[b][:]), t,
                                          free["gw"][0], free["gw"][1])
                                give(b, ev)
                        tok["wal"] = ev
                    add(Job(mmw))
            dep = [done[n] for n in range(NT)]

        base = 9
        prev_agg = []
        for f in range(2):
            hZ = base + f
            for n in range(NT):
                def postz(box, n=n):
                    tl, th = split_z(n, bank[box["b"]][0:T, :], None, box["t"])
                    give(box["b"], tl)
                add(Job(mm_x(hZ), prep_x(xT_d[2][n], lambda n=n: (tok["xT", 2, n],)), postz, after=dep[n], w=hZ))
                if f == 0 and n == 3:
                    jb = add(Job(bcast_job(PQ[0][1]), after=dep[-1]))
            for d in range(NT):
                def late(box, d=d, f=f):
                    box["r"] = load_r(x_d[1][d][:, f * HW:(f + 1) * HW], tok["xd", 1, d])

                def post(box, d=d, f=f):
                    b, t = box["b"], box["t"]
                    r, tr = box["r"]
                    if f == 0:
                        q = V.op(lambda: ve.tensor_scalar(RS[:, d:d + 1], bank[7][0:T, 0:1], 1e-5, None, ALU.add), t)
                        bank_free[7] = q
                        t = V.op(lambda: ve.reciprocal(RS[:, d:d + 1], RS[:, d:d + 1]), q)
                    i, j = nxt("u", 2), nxt("u", 2)
                    tv = V.op(lambda: ve.tensor_scalar(U[i][:], bank[b][0:T, :], RS[:, d:d + 1], None, ALU.mult), t,
                              free["u"][i])
                    give(b, tv)
                    tm = V.op(lambda: ve.tensor_scalar(U[j][:], U[i][:], 0.0, None, ALU.min), tv, free["u"][j])
                    te_ = A.op(lambda: ac.activation(U[j][:], U[j][:], ACT.Exp), tm)
                    t1 = V.op(lambda: ve.scalar_tensor_tensor(U[i][:], U[i][:], 0.0, U[j][:], ALU.max, ALU.add), te_)
                    free["u"][j] = t1
                    o = G[:, d, :] if f == 0 else R[r][:]
                    t2 = V.op(lambda: ve.scalar_tensor_tensor(o, U[i][:], -1.0, R[r][:], ALU.add, ALU.add), t1, tr)
                    free["u"][i] = t2
                    if f == 0:
                        free["r"][r] = t2
                    else:
                        box["ln"] = norm(G[:, d, :], R[r][:], (t2,))
                        free["r"][r] = box["ln"][1]
                job = Job(mm_m("att", rowsum=(f == 0)), prep_m("att", d), post, after=jb, late=late)
                if f == 1:
                    job.tail = (lambda box, d=d: finish_tile(box, d, 2)(box))
                j = add(job)
                if f == 1:
                    prev_agg.append(j)

        dep = prev_agg
        for f in range(2):
            hZ = 11 + f
            for n in range(NT):
                def postz(box, n=n):
                    tl, th = split_z(n, bank[box["b"]][0:T, :], D3, box["t"], tok["deg"])
                    give(box["b"], tl)
                add(Job(mm_x(hZ), prep_x(xT_d[3][n], lambda n=n: (tok["xT", 3, n],)), postz, after=dep[n], w=hZ))
            for d in range(NT):
                prep = prep_m("loop", d)
                if d == 0:
                    def load_first(box, f=f, load=prep[0]):
                        load_b(b3[f * HW:(f + 1) * HW])
                        load(box)
                    prep = (load_first,) + prep[1:]

                def late(box, d=d, f=f):
                    box["r"] = load_r(x_d[2][d][:, f * HW:(f + 1) * HW], tok["xd", 2, d])

                def post(box, d=d, f=f):
                    b, t = box["b"], box["t"]
                    r, tr = box["r"]
                    i = nxt("u", 2)
                    tv = V.op(lambda: ve.scalar_tensor_tensor(U[i][:], bank[b][0:T, :], D3[:, d:d + 1], B[0:T, :],
                                                             ALU.mult, ALU.add), t, tok["b"], free["u"][i])
                    give(b, tv)
                    free["b"] = tv
                    o = G[:, d, :] if f == 0 else R[r][:]
                    t2 = V.op(lambda: ve.scalar_tensor_tensor(o, U[i][:], 0.0, R[r][:], ALU.max, ALU.add), tv, tr)
                    free["u"][i] = t2
                    if f == 0:
                        free["r"][r] = t2
                    else:
                        ln = norm(G[:, d, :], R[r][:], (t2,))
                        free["r"][r] = ln[1]
                        w = s_xo[ln[2]].dma(S, sy, out[d * T:(d + 1) * T, :], XO[ln[2]][:], ln[0], ln[1])
                        free["xo"][ln[2]] = [w]
                        tok["out"] = w
                add(Job(mm_m("loop"), prep, post, late=late))

        box = [dict() for _ in jobs]
        final = {job.w: j for j, job in enumerate(jobs) if job.w is not None}
        at = {"load": 0, "first": 0, "second": 0, "tail": 0}

        def do_tails(upto):
            while at["tail"] <= upto:
                j = at["tail"]
                at["tail"] += 1
                if jobs[j].tail:
                    jobs[j].tail(box[j])

        def stage(name, upto, must, below):
            while at[name] <= min(upto, below - 1, len(jobs) - 1):
                j = at[name]
                if name == "load" and j > must and j - 1 > at["second"]:
                    return
                if name == "load" and jobs[j].after >= at["tail"]:
                    if j > must:
                        return
                    do_tails(jobs[j].after)
                fn = {"load": jobs[j].load, "first": jobs[j].first, "second": jobs[j].second}[name]
                at[name] += 1
                if fn:
                    fn(box[j])

        n = len(jobs)
        for j, job in enumerate(jobs):
            stage("load", j, j, n)
            stage("first", j, j, n)
            stage("second", j, j, n)
            job.mm(box[j])
            do_tails(j - 2)
            stage("first", j + 2, j, at["load"])
            stage("load", j + 3, j, n)
            stage("second", j + 2, j, at["first"])
            stage("load", j + 3, j, n)
            if j + 3 < n and jobs[j + 3].w is not None and final[jobs[j + 3].w] == j + 3 and jobs[j + 3].w < 12:
                stage_slabs(jobs[j + 3].w + 1)
            if job.post:
                job.post(box[j])
            if j + 1 < n and jobs[j + 1].late:
                jobs[j + 1].late(box[j + 1])
            if job.w is not None and final[job.w] == j:
                may_load(job.w)
        do_tails(n - 1)
        S.wait(tok["out"], *[(s.sem, s.n) for s in
                             [s_xt, s_at] + s_xo + s_a + s_r + s_g])

        block = ctx.enter_context(nc.Block())
        for q, name in ((PE, "tensor"), (V, "vector"), (A, "scalar"), (P, "gpsimd"), (S, "sync")):
            def body(eng, q=q):
                q.emit(eng)
            {"tensor": block.tensor, "vector": block.vector, "scalar": block.scalar, "gpsimd": block.gpsimd,
             "sync": block.sync}[name](body)


_OUTS = [((N, D), "float32")]


def kernel(**inputs):
    import numpy as _np
    import concourse.bacc as _bacc
    from concourse import mybir as _mybir
    from concourse.bass_utils import run_bass_kernel_spmd as _run

    nc = _bacc.Bacc("TRN2", target_bir_lowering=False, num_devices=1)
    get = {k: _np.asarray(v) for k, v in inputs.items()}
    x = get["x"]
    win = _np.array([[lo * T for lo, hi in windows()], [(hi + 1) * T - 1 for lo, hi in windows()]], _np.float32)
    win = _np.tile(win.reshape(1, 2 * NC), (T, 1))
    arrays = {
        "xT": x.reshape(NT, T, 8, 128).transpose(0, 3, 2, 1).reshape(NT, 128, 8 * T),
        "x": x,
        "es": get["src"].reshape(NC, T).T,
        "ed": get["dst"].reshape(NC, T).T,
        "win": win,
        "W1": get["L0_gnn_W1"], "b1": get["L0_gnn_b1"], "gw": get["L0_gnn_gate_w"], "gb": get["L0_gnn_gate_b"],
        "Ws0": get["L1_gnn_W_self0"], "Wn0": get["L1_gnn_W_neigh0"], "b0": get["L1_gnn_b0"],
        "Ws1": get["L1_gnn_W_self1"], "Wn1": get["L1_gnn_W_neigh1"], "bb1": get["L1_gnn_b1"],
        "W2": get["L2_gnn_W"], "a2": get["L2_gnn_a"], "W3": get["L3_gnn_W"], "b3": get["L3_gnn_b"],
    }
    args, named = [], {}
    for name, a in arrays.items():
        a = _np.ascontiguousarray(a)
        named[f"in_{name}"] = a
        args.append(nc.dram_tensor(f"in_{name}", a.shape, _mybir.dt.from_np(a.dtype), kind="ExternalInput").ap())
    o = nc.dram_tensor("out_0", _OUTS[0][0], _mybir.dt.float32, kind="ExternalOutput").ap()
    gnn_program(nc, *args, o)
    r = _run(nc, [named], core_ids=[0])
    return r.results[0]["out_0"]
```

```python
import numpy as np
import concourse.bass as bass
from concourse import mybir
from contextlib import ExitStack

N, D, E = 1250, 1024, 21250
T = 125
NT = N // T
NC = E // T
HW = 512
PER = NC // NT
MARGIN = 2
NSLOT = 8


def windows():
    out = []
    for c in range(NC):
        lo = max(0, -((PER - 1 + MARGIN - c) // PER))
        hi = min(NT - 1, (c + MARGIN) // PER)
        out.append((lo, hi))
    return out


class Queue:

    def __init__(self, sem):
        self.sem, self.n, self.items = sem, 0, []

    def op(self, fn, *waits):
        self.n += 1
        self.items.append((fn, waits, (self.sem, 1)))
        return (self.sem, self.n)

    def quiet(self, fn, *waits):
        self.items.append((fn, waits, None))

    def wait(self, *waits):
        self.items.append((None, waits, None))

    def emit(self, eng):
        seen = {}
        for fn, waits, inc in self.items:
            for w in waits:
                if w is None:
                    continue
                sem, v = w
                if seen.get(id(sem), 0) < v:
                    eng.wait_ge(sem, v)
                    seen[id(sem)] = v
            if fn is None:
                continue
            ins = fn()
            if inc is not None:
                ins.then_inc(*inc)


class Slot:

    def __init__(self, sem):
        self.sem, self.n = sem, 0

    def dma(self, q, eng, out, in_, *waits):
        self.n += 16
        q.items.append((lambda: eng.dma_start(out, in_), waits, (self.sem, 16)))
        return (self.sem, self.n)


class Job:

    def __init__(self, mm, prep=(None, None, None), post=None, tail=None, after=-1, w=None, late=None, mid=None,
                 pre=None, after_post=-1):
        self.eager, self.soon, self.after_mid = False, None, None
        self.mid, self.pre, self.after_post = mid, pre, after_post
        self.load, self.first, self.second = prep
        self.mm, self.post, self.tail, self.after, self.w, self.late = mm, post, tail, after, w, late


def gnn_program(nc, xT, x, es, ed, win, W1, b1, gw, gb, Ws0, Wn0, b0, Ws1, Wn1, bb1, W2, a2, W3, b3, out):
    f32, fr, bf, f16 = mybir.dt.float32, mybir.dt.float32r, mybir.dt.bfloat16, mybir.dt.float16
    i16, i32 = mybir.dt.int16, mybir.dt.int32
    ALU, ACT = mybir.AluOpType, mybir.ActivationFunctionType
    AXX = mybir.AxisListType.X
    FMAX = 3.0e38

    def dram(name, shape, dt):
        return nc.dram_tensor(name, shape, dt, kind="Internal").ap()

    a_d = dram("a_d", (NT, T, NT * T), i16)
    at_d = dram("at_d", (NT, T, NT * T), i16)
    x_d = [dram(f"x_d{i}", (NT, T, D), f32) for i in range(3)]
    xT_d = [xT] + [dram(f"xT_d{i}", (NT, 128, 8 * T), f32) for i in range(1, 4)]
    hT_d = dram("hT_d", (NT, 128, 8 * T), f32)
    yl_d = dram("yl_d", (NT, T, HW), f32)
    m_d = dram("m_d", (NT, T, NT * T), f32)

    ctx = ExitStack()
    with ctx:
        def sb(name, shape, dt, c=None):
            return (c or ctx).enter_context(nc.sbuf_tensor(name, shape, dt))

        def sem(name):
            return ctx.enter_context(nc.semaphore(name))

        PE, V, A, P, S = (Queue(sem(f"q_{n}")) for n in ("pe", "dve", "act", "pool", "sync"))
        te, ve, ac, po, sy = nc.tensor, nc.vector, nc.scalar, nc.gpsimd, nc.sync

        wh = [sb(f"wh{i}", [128, HW], fr) for i in range(NSLOT)]
        wl = [sb(f"wl{i}", [128, HW], fr) for i in range(NSLOT)]
        ws = [sb(f"ws{i}", [128, HW], f32) for i in range(2)]
        xs = [sb(f"xs{i}", [128, 8, T], f32) for i in range(2)]
        xh = [sb(f"xh{i}", [128, 8, T], fr) for i in range(2)]
        xl = [sb(f"xl{i}", [128, 8, T], fr) for i in range(2)]
        ident = sb("ident", [128, 128], f32)
        ones = sb("ones", [128, 4], f32)
        DEG = sb("DEG", [T, NT], f32)
        DEG3 = sb("DEG3", [T, NT, 3], f32)
        DD, DR, DT = (sb(f"DD{i}", [T, 2, NT], f32) for i in range(3))
        DIS, D3 = DR[:, 0, :], DR[:, 1, :]
        DEGI = sb("DEGI", [T, NT], f32)
        sm = sb("sm", [128, 16], f32)
        flags = sb("flags", [1, 2], i32)
        WC = sb("WC", [128, 2, 8], f32)
        WP = sb("WP", [128, 2, 2, 8], f32)
        GB = sb("GB", [128, 4], f32)
        PQ = [[sb(f"P{i}", [T, NT], f32), sb(f"Q{i}", [T, NT], f32)] for i in range(2)]
        RS = sb("RS", [T, NT], f32)
        st = [sb(f"st{i}", [T, 12], f32) for i in range(2)]
        mv = [sb(f"mv{i}", [T, 6], f32) for i in range(2)]
        bank = [ctx.enter_context(nc.psum_tensor(f"bank{i}", [128, HW], f32)) for i in range(8)]
        bank_free = [None] * 8
        idle = list(range(6))

        def take():
            return idle.pop(0)

        def give(b, t):
            bank_free[b] = t
            idle.append(b)

        free = {"gw": [None, None], "ar": [None] * 2, "r": [None] * 4, "u": [None] * 2, "t": [(), ()],
                "m": [None] * 3, "xo": None, "xt": None, "b": None, "pb": [None] * NT, "pq": [None] * 2, "st": [None] * 2, "sum": [None] * 2}
        cnt = {"ar": 0, "m": 0, "r": 0, "u": 0, "t": 0, "st": 0}
        halves = []
        wsl = [Slot(sem(f"s_ws{i}")) for i in range(6)]
        slot_free = [()] * NSLOT
        w_tok = {}
        nslab = [0]

        def add_half(ap):
            halves.append(ap)
            return len(halves) - 1

        stages = []
        staged = []
        nstaged = [0]

        def stage_slabs(h):
            wide = 2 <= h <= 9
            while nstaged[0] < 8 * min(h + 1, len(halves)):
                pick = [x for x in stages[:6 if wide else 2] if not x["busy"]]
                if not pick:
                    return
                x = min(pick, key=lambda x: x["turn"])
                g = nstaged[0]
                nstaged[0] += 1
                k = g % 8
                waits = [x["free"]] + (list(free["t"][x["t"]]) if x["t"] is not None else [])
                t = x["slot"].dma(S, sy, x["ap"], halves[g // 8][k * 128:(k + 1) * 128, :], *waits)
                x["busy"], x["turn"] = True, g
                staged.append((g, x, t))

        def split_slab():
            g, x, t = staged.pop(0)
            s = g % NSLOT
            th = A.op(lambda: ac.copy(wh[s][:], x["ap"]), t, *slot_free[s])
            q, e = (P, po) if g % 2 or g < 8 else (V, ve)
            tl = q.op(lambda: e.tensor_tensor(wl[s][:], x["ap"], wh[s][:].bitcast(f32), ALU.subtract), t, th,
                      *slot_free[s])
            x["free"], x["busy"] = tl, False
            if x["t"] is not None:
                free["t"][x["t"]] = (*free["t"][x["t"]], tl)
            w_tok[g // 8, g % 8] = (s, th, tl)

        def may_load(done, j=0, first_use=None):
            n = 0
            while nslab[0] < 8 * len(halves):
                if nslab[0] >= NSLOT and (nslab[0] - NSLOT) // 8 > done:
                    return
                far = first_use and first_use[nslab[0] // 8] - j > 5 + 8 - nslab[0] % 8
                if far and (n == 2 or not staged or j % 2 == 0):
                    if j % 2 == 0:
                        stage_slabs(nslab[0] // 8)
                    return
                n += 1
                if not staged:
                    stage_slabs(nslab[0] // 8)
                split_slab()
                nslab[0] += 1
                if not far:
                    stage_slabs((nslab[0] - 1) // 8)

        xsl = [Slot(sem(f"s_xs{i}")) for i in range(2)]
        x_turn = [0]
        xs_free = [(), ()]
        x_free = [None, None]

        def prep_x(src, ready):
            def load(box):
                i = x_turn[0] % 2
                x_turn[0] += 1
                t = xsl[i].dma(S, sy, xs[i][:], src.rearrange("p (k n) -> p k n", k=8), *xs_free[i], *ready())
                box["x"] = (i, t)

            def first(box):
                i, t = box["x"]
                box["x"] = (i, t, A.op(lambda: ac.copy(xh[i][:], xs[i][:]), t, x_free[i]))

            def second(box):
                i, t, th = box["x"]
                tl = V.op(lambda: ve.tensor_tensor(xl[i][:], xs[i][:], xh[i][:].bitcast(f32), ALU.subtract), t, th,
                          x_free[i])
                xs_free[i] = (tl,)
                box["x"] = (i, th, tl)
            return load, first, second

        def mm_x(h):
            def mm(box):
                i, th, tl = box["x"]
                b = take()
                PE.wait(th, tl, bank_free[b])
                for k in range(8):
                    s, wth, wtl = w_tok[h, k]
                    PE.wait(wth, wtl)
                    o = bank[b][0:T, :]
                    PE.quiet(lambda k=k, s=s: te.matmul(o, xh[i][:, k, :], wh[s][:], start=(k == 0), stop=False))
                    PE.quiet(lambda k=k, s=s: te.matmul(o, xh[i][:, k, :], wl[s][:], start=False, stop=False))
                    f = (lambda k=k, s=s: te.matmul(o, xl[i][:, k, :], wh[s][:], start=False, stop=(k == 7)))
                    if k < 7:
                        PE.quiet(f)
                t = PE.op(f)
                x_free[i] = t
                for k in range(8):
                    slot_free[w_tok[h, k][0]] = (t,)
                box["b"], box["t"] = b, t
            return mm

        hW1 = add_half(W1)
        for wn, wsf in ((Wn0, Ws0), (Wn1, Ws1)):
            for f in range(2):
                add_half(wn[:, f * HW:(f + 1) * HW])
                add_half(wsf[:, f * HW:(f + 1) * HW])
        for w in (W2, W3):
            for f in range(2):
                add_half(w[:, f * HW:(f + 1) * HW])

        WIN = windows()
        c_first = {b: min(c for c in range(NC) if WIN[c][0] <= b <= WIN[c][1]) for b in range(NT)}
        c_last = {b: max(c for c in range(NC) if WIN[c][0] <= b <= WIN[c][1]) for b in range(NT)}
        PC = [(0, 417), (417, 834), (834, 1250)]

        Zh = sb("Zh", [T, NT, HW], fr)
        Zl = sb("Zl", [T, NT, HW], fr)
        G = sb("G", [T, NT, HW], f32)
        GW = sb("GW", [128, 2, D], f32)
        B = sb("B", [128, HW], f32)
        GSF = sb("GSF", [128, D], bf)
        GS, GS2 = GSF[0:T, :], GSF[:, 0:HW]

        ca = ExitStack()
        ei = sb("ei", [T, 2, NC], i32, ca)
        ef = sb("ef", [T, 2, NC], f32, ca)
        wn_ = sb("wn_", [T, 2, NC], f32, ca)
        wt = sb("wt", [T, 2, NC], f32, ca)
        iot = sb("iot", [T, N], f16, ca)
        oS = [sb(f"oS{i}", [T, N], bf, ca) for i in range(4)]
        oD = [sb(f"oD{i}", [T, 2 * T], bf, ca) for i in range(4)]
        zz = sb("zz", [T, HW], bf, ca)
        AT = sb("AT", [T, NT, N], i16, ca)
        Af = [sb(f"Af{i}", [T, N], f32, ca) for i in range(2)]
        A16 = [sb(f"A16{i}", [T, NT, T], i16, ca) for i in range(2)]
        ca.close()

        Mh = [sb(f"Mh{i}", [T, NT, T], fr) for i in range(3)]
        Ml = [sb(f"Ml{i}", [T, NT, T], fr) for i in range(3)]
        TF = [sb(f"Tt{i}", [128, NT * T], f32) for i in range(2)]
        Tt = [t[0:T, :].rearrange("p (a c) -> p a c", c=T) for t in TF]
        Ar = [sb(f"Ar{i}", [T, NT, T], i16) for i in range(2)]
        PB = sb("PB", [T, NT, T], f32)
        RF = [sb(f"R{i}", [128, HW], f32) for i in range(4)]
        UF = [sb(f"U{i}", [128, HW], f32) for i in range(2)]
        R, U = [r[0:T, :] for r in RF], [u[0:T, :] for u in UF]
        XO = [sb(f"XO{i}", [T, D], f32) for i in range(2)]
        XT = sb("XT", [128, 8, T], f32)


        s_e, s_c = Slot(sem("s_e")), Slot(sem("s_c"))
        te_ = s_e.dma(S, sy, ei[:, 0, :], es)
        te_ = s_e.dma(S, sy, ei[:, 1, :], ed)
        te_ = s_e.dma(S, sy, wn_[:], win.rearrange("p (a c) -> p a c", a=2))
        tc_ = s_c.dma(S, sy, GB[:], gb.rearrange("k o -> o k").partition_broadcast(128).rearrange("p o k -> p (o k)"))

        ti = P.op(lambda: po.iota(iot[:], [[1, N]], base=0, channel_multiplier=0, allow_small_or_imprecise_dtypes=True))
        t0 = P.op(lambda: po.memset(ident[:], 0.0))
        tid = P.op(lambda: po.affine_select(out=ident[:], in_=ident[:], compare_op=ALU.not_equal, fill=1.0, base=0,
                                            pattern=[[-1, 128]], channel_multiplier=1), t0)
        to = P.op(lambda: po.memset(ones[:], 1.0))
        tz = P.op(lambda: po.memset(zz[:], 0.0))

        t1 = V.op(lambda: ve.tensor_copy(ef[:], ei[:]), te_)
        t2 = V.op(lambda: ve.tensor_tensor(wt[:, 0, :], wn_[:, 0, :], ef[:, 1, :], ALU.subtract), t1)
        t3 = V.op(lambda: ve.tensor_tensor(wt[:, 1, :], ef[:, 1, :], wn_[:, 1, :], ALU.subtract), t1)
        t4 = V.op(lambda: ve.reduce_max(sm[0:T, 0:1], wt[:].rearrange("p a c -> p (a c)"), AXX), t2, t3)
        t5 = V.op(lambda: ve.tensor_scalar(sm[0:T, 1:2], sm[0:T, 0:1], 0.0, None, ALU.is_gt), t4)
        t6 = PE.op(lambda: te.matmul(bank[7][0:1, 0:1], sm[0:T, 1:2], ones[0:T, 0:1], start=True, stop=True), t5, to)
        tflag = V.op(lambda: ve.tensor_copy(flags[0:1, 0:1], bank[7][0:1, 0:1]), t6)

        x_ahead = [dict(), dict()]
        for n in range(2):
            for part in prep_x(xT_d[0][n], lambda: ()):
                part(x_ahead[n])

        for i in range(6):
            stages.append({"slot": wsl[i], "ap": ws[i][:] if i < 2 else TF[i // 2 - 1][:, (i % 2) * HW:(i % 2) * HW + HW],
                           "t": None if i < 2 else i // 2 - 1, "free": None, "busy": False, "turn": -1})
        may_load(-1)

        fS, fP, fE = sem("fS"), sem("fP"), sem("fE")
        gS, gP, gB, gE = sem("gS"), sem("gP"), sem("gB"), sem("gE")

        def dve_build():
            v = ve.value_load(flags[0:1, 0:1], min_val=0, max_val=T)
            with ve.If(v < 1):
                for c in range(NC):
                    i = c % 4
                    lo, hi = WIN[c]
                    if c >= 4:
                        ve.wait_ge(fP, c - 3)
                    ve.tensor_scalar(oS[i][:], iot[:], ef[:, 0, c:c + 1], None, ALU.is_equal).then_inc(fS, 1)
                    n = (hi - lo + 1) * T
                    ve.tensor_scalar(oD[i][:, 0:n], iot[:, lo * T:lo * T + n], ef[:, 1, c:c + 1], None,
                                     ALU.is_equal).then_inc(fS, 1)
            with ve.Else():
                for b in range(NT):
                    with ve.Fori(0, NC) as c:
                        ve.wait_ge(gP, 1)
                        ve.sem_clear(gP)
                        ve.tensor_scalar(oS[0][:], iot[:], ef[:, 0, bass.ds(c, 1)], None, ALU.is_equal).then_inc(gS, 1)
                        ve.tensor_scalar(oD[0][:, 0:T], iot[:, b * T:(b + 1) * T], ef[:, 1, bass.ds(c, 1)], None,
                                         ALU.is_equal).then_inc(gS, 1)

        def pe_build():
            v = te.value_load(flags[0:1, 0:1], min_val=0, max_val=T)
            with te.If(v < 1):
                for c in range(NC):
                    i = c % 4
                    lo, hi = WIN[c]
                    te.wait_ge(fS, 2 * (c + 1))
                    for b in range(lo, hi + 1):
                        if c == c_first[b] and b >= 2:
                            te.wait_ge(fE, b - 1)
                        for j, (u, w) in enumerate(PC):
                            m = te.matmul(bank[3 * (b % 2) + j][0:T, 0:w - u], oD[i][:, (b - lo) * T:(b - lo + 1) * T],
                                          oS[i][:, u:w], start=(c == c_first[b]), stop=(c == c_last[b]))
                    m.then_inc(fP, 1)
            with te.Else():
                te.sem_inc(gP, 1)
                for b in range(NT):
                    if b:
                        te.wait_ge(gE, b)
                    for j, (u, w) in enumerate(PC):
                        te.matmul(bank[j][0:T, 0:w - u], zz[:, 0:T], zz[:, 0:w - u], start=True, stop=False)
                    with te.Fori(0, NC) as c:
                        te.wait_ge(gS, 2)
                        te.sem_clear(gS)
                        for j, (u, w) in enumerate(PC):
                            m = te.matmul(bank[j][0:T, 0:w - u], oD[0][:, 0:T], oS[0][:, u:w], start=False, stop=False)
                        m.then_inc(gP, 1)
                    for j, (u, w) in enumerate(PC):
                        m = te.matmul(bank[j][0:T, 0:w - u], zz[:, 0:T], zz[:, 0:w - u], start=False, stop=True)
                    m.then_inc(gB, 1)

        def act_build():
            v = ac.value_load(flags[0:1, 0:1], min_val=0, max_val=T)
            with ac.If(v < 1):
                for b in range(NT):
                    ac.wait_ge(fP, c_last[b] + 1)
                    for j, (u, w) in enumerate(PC):
                        m = ac.activation(AT[:, b, u:w], bank[3 * (b % 2) + j][0:T, 0:w - u], ACT.Copy,
                                          accum_out=DEG3[:, b, j:j + 1])
                    m.then_inc(fE, 1)
            with ac.Else():
                for b in range(NT):
                    ac.wait_ge(gB, b + 1)
                    for j, (u, w) in enumerate(PC):
                        m = ac.activation(AT[:, b, u:w], bank[j][0:T, 0:w - u], ACT.Copy,
                                          accum_out=DEG3[:, b, j:j + 1])
                    m.then_inc(*((gE, 1) if b < NT - 1 else (fE, NT - 1)))

        V.wait(t1, ti, tflag)
        V.quiet(lambda: (dve_build(), None)[1])
        PE.wait(tz, tflag)
        PE.quiet(lambda: (pe_build(), None)[1])
        A.wait(tflag)
        A.quiet(lambda: (act_build(), None)[1])
        tA = A.op(lambda: ac.copy(sm[0:1, 8:9], ident[0:1, 0:1]), tid)
        PE.op(lambda: te.matmul(bank[7][0:1, 0:1], ones[0:1, 0:1], ones[0:1, 0:1], start=True, stop=True), tflag)
        for b in range(6):
            bank_free[b] = (fE, NT - 1) if b < 3 else tA
        bank_free[7] = tflag

        s_at = Slot(sem("s_at"))
        s_a = [Slot(sem(f"s_a{i}")) for i in range(2)]
        af_free = [None, None]
        a16_free = [None, None]
        af_tok = [None] * NT
        big = {}

        def counts_float(b):
            i = b % 2
            af_tok[b] = A.op(lambda: ac.copy(Af[i][:], AT[:, b, :]), tA, af_free[i])

        def counts_out(b):
            i = b % 2
            for u, w in ((0, 4), (4, 8), (8, 10)):
                bk = take()
                PE.wait(af_tok[b], bank_free[bk], tid)
                for j in range(u, w):
                    fn = (lambda j=j, u=u, bk=bk: te.transpose(bank[bk][0:T, (j - u) * T:(j - u + 1) * T],
                                                              Af[i][:, j * T:(j + 1) * T], ident[0:T, 0:T]))
                    tt = PE.op(fn)
                ev = A.op(lambda u=u, w=w, bk=bk: ac.copy(
                    A16[i][:, u:w, :], bank[bk][0:T, 0:(w - u) * T].rearrange("p (a c) -> p a c", c=T)), tt, a16_free[i])
                give(bk, ev)
            af_free[i] = tt
            a16_free[i] = s_a[i].dma(S, sy, a_d[b].rearrange("p (a c) -> p a c", c=T), A16[i][:], ev)

        def degrees():
            tok["degs"] = dd = V.op(lambda: ve.reduce_sum(DEG[:], DEG3[:], AXX), tA)
            t = V.op(lambda: ve.tensor_scalar(DD[:, 0, :], DEG[:], 1.0, None, ALU.max), dd)
            t = V.op(lambda: ve.tensor_scalar(DD[:, 1, :], DEG[:], 1.0, None, ALU.add), dd)
            V.op(lambda: ve.reciprocal(DEGI[:], DD[:, 0, :]), t)
            tok["deg"] = rsqrt(DR[:], DD[:], DT[:], (V.sem, V.n))

        def leave_build(_):
            dd = tok["degs"]
            t = V.op(lambda: ve.reduce_max(sm[0:T, 2:3], DEG[:], AXX), dd)
            t = V.op(lambda: ve.tensor_scalar(sm[0:T, 3:4], sm[0:T, 2:3], 4096.0, None, ALU.is_gt), t)
            t = PE.op(lambda: te.matmul(bank[7][0:1, 0:1], sm[0:T, 3:4], ones[0:T, 0:1], start=True, stop=True), t)
            t = V.op(lambda: ve.tensor_copy(flags[0:1, 1:2], bank[7][0:1, 0:1]), t)
            bank_free[7] = t
            PE.quiet(lambda: big.update(v=te.value_load(flags[0:1, 1:2], min_val=0, max_val=T)), t)
            V.quiet(lambda: big.update(dve=ve.value_load(flags[0:1, 1:2], min_val=0, max_val=T)), t)
            ends = [(PE.sem, PE.n), (V.sem, V.n), (A.sem, A.n), (P.sem, P.n), (s_at.sem, s_at.n),
                    a16_free[0], a16_free[1]]
            for q in (PE, V, A, P, S):
                q.wait(*ends)


        jobs = []
        s_gw = [Slot(sem(f"s_gw{i}")) for i in range(2)]
        s_ar = [Slot(sem(f"s_ar{i}")) for i in range(2)]
        s_r = [Slot(sem(f"s_r{i}")) for i in range(4)]
        s_b = Slot(sem("s_b"))
        s_t = [Slot(sem(f"s_t{i}")) for i in range(2)]
        s_xo, s_xt = [Slot(sem(f"s_xo{i}")) for i in range(2)], Slot(sem("s_xt"))
        tok = {}

        def nxt(name, n):
            i = cnt[name] % n
            cnt[name] += 1
            return i

        def load_r(src, *waits):
            i = nxt("r", 4)
            return i, s_r[i].dma(S, sy, R[i][:], src, free["r"][i], *waits)

        def load_b(src):
            tok["b"] = s_b.dma(S, sy, B[:], src.rearrange("(o c) -> o c", o=1).partition_broadcast(128).rearrange("p o c -> p (o c)"), free["b"])

        def edge_weights(kind, i, d, par, lo, hi, t0):
            col = PQ[par][1] if kind == "gate" else PQ[0][0]
            rd = (tok["pb", d], tok["pq", par, hi - 1])
            fn = ACT.Tanh if kind == "gate" else ACT.Identity
            v = Tt[i][:, lo:hi, :]
            if hi - lo == 1:
                t = A.op(lambda: ac.activation(Tt[i][:, lo, :], PB[:, d, :], fn, bias=col[:, lo:hi]), *t0, *rd)
                free["pb"][d] = free["pq"][par] = t
            else:
                row = PB[:, d, :].unsqueeze(1).to_broadcast([T, hi - lo, T])
                cb = col[:, lo:hi].unsqueeze(2).to_broadcast([T, hi - lo, T])
                t = P.op(lambda: po.tensor_tensor(v, row, cb, ALU.add), *t0, *rd)
                free["pb"][d] = free["pq"][par] = t
                if kind == "gate":
                    t = A.op(lambda: ac.activation(v, v, ACT.Tanh), t)
            if kind == "att":
                t = V.op(lambda: ve.scalar_tensor_tensor(v, v, 0.1, v, ALU.mult, ALU.max), t)
                t = A.op(lambda: ac.activation(v, v, ACT.Exp, scale=-1.0), t)
            return t

        def times_counts(kind, i, r, lo, hi, t, ta):
            v, a = Tt[i][:, lo:hi, :], Ar[r][:, lo:hi, :]
            if kind == "gate":
                return V.op(lambda: ve.tensor_tensor(v, v, a, ALU.mult), t, ta)
            return V.op(lambda: ve.scalar_tensor_tensor(v, v, FMAX, a, ALU.min, ALU.mult), t, ta)

        def load_counts(src, d):
            r = nxt("ar", 2)
            return r, s_ar[r].dma(S, sy, Ar[r][:], src[d].rearrange("p (a c) -> p a c", c=T), free["ar"][r])

        s_lo, n_lo = sem("s_lo"), [0]

        def prep_m(kind, d, par=0, early=False):
            def times(box):
                M, t, name, k = box["in"]
                r, ta = box.pop("ar")
                t = free["ar"][r] = times_counts(kind, k, r, 0, NT, t, ta)
                box["in"] = (M, t, name, k)

            def load(box):
                if kind == "kept":
                    i = nxt("t", 2)
                    ta = s_t[i].dma(S, sy, TF[i][0:T, :], m_d[d], *free["t"][i], tok["kept", d])
                    box["in"] = (Tt[i], ta, "t", i)
                    return
                r, ta = load_counts(at_d if kind == "att" else a_d, d)
                if kind in ("gate", "att"):
                    i = nxt("t", 2)
                    box["in"] = (Tt[i], edge_weights(kind, i, d, par, 0, NT, free["t"][i]), "t", i)
                    box["ar"] = (r, ta)
                    if early:
                        times(box)
                else:
                    if kind == "loop":
                        ta = V.op(lambda: ve.tensor_tensor(Ar[r][:, d, :], Ar[r][:, d, :], ident[0:T, 0:T], ALU.add), ta)
                    box["in"] = (Ar[r], ta, "ar", r)

            def first(box):
                if "ar" in box:
                    times(box)
                M, t, name, k = box["in"]
                i = nxt("m", 3)
                th = A.op(lambda: ac.copy(Mh[i][:], M[:]), t, free["m"][i])
                if kind == "att":
                    box["kept"] = tok["kept", d] = s_t[k].dma(A, ac, m_d[d], TF[k][0:T, :], t)
                box["m"] = (i, [th] * NT)

            def second(box):
                M, t, name, k = box["in"]
                i, th = box["m"]
                if name == "ar":
                    def lower():
                        with ve.If(big["dve"] > 0):
                            ve.tensor_tensor(Ml[i][:], M[:], Mh[i][:].bitcast(f32), ALU.subtract).then_inc(s_lo, 1)
                        with ve.Else():
                            ve.sem_inc(s_lo, 1)
                    V.quiet(lambda: (lower(), None)[1], th[0], t, free["m"][i])
                    n_lo[0] += 1
                    tl = free[name][k] = (s_lo, n_lo[0])
                    box["m"] = (i, th, [tl] * NT)
                    return
                tl = V.op(lambda: ve.tensor_tensor(Ml[i][:], M[:], Mh[i][:].bitcast(f32), ALU.subtract), th[0], t,
                          free["m"][i])
                if kind == "att":
                    s = GW[0:T, d % 2, 0:5 * T].rearrange("p (a c) -> p a c", c=T)
                    box["half"] = P.op(lambda: po.tensor_tensor(s, Tt[k][:, 0:5, :], Tt[k][:, 5:10, :], ALU.add), t,
                                       free["sum"][d % 2])
                    box["sum"] = P.op(lambda: po.tensor_tensor(s[:, 0:2, :], s[:, 0:2, :], s[:, 2:4, :], ALU.add),
                                      box["half"])
                free[name][k] = (tl, box.get("kept"), box.get("half"))
                box["m"] = (i, th, [tl] * NT)
            return load, first, second

        def build_part(box, d, par, part):
            lo, hi = ((0, NT - 1), (NT - 1, NT))[part]
            if part == 0:
                box["r"] = load_counts(a_d, d)
                box["i"], box["k"] = nxt("t", 2), nxt("m", 3)
                box["m"] = (box["k"], [None] * NT, [None] * NT)
            (r, ta), i, k = box["r"], box["i"], box["k"]
            t = edge_weights("gate", i, d, par, lo, hi, free["t"][i])
            t = times_counts("gate", i, r, lo, hi, t, ta)
            th = A.op(lambda: ac.copy(Mh[k][:, lo:hi, :], Tt[i][:, lo:hi, :]), t, free["m"][k])
            tl = V.op(lambda: ve.tensor_tensor(Ml[k][:, lo:hi, :], Tt[i][:, lo:hi, :], Mh[k][:, lo:hi, :].bitcast(f32),
                                               ALU.subtract), th, free["m"][k])
            for s in range(lo, hi):
                box["m"][1][s], box["m"][2][s] = th, tl
            if part:
                free["ar"][r], free["t"][i] = t, (tl,)

        def mm_m(kind, d=0, rowsum=False, signal=False):
            def mm(box):
                i, th, tl = box["m"]
                b = take()
                o = bank[b][0:T, :]
                PE.wait(bank_free[b])
                full = kind in ("gate", "att", "kept")
                for s in range(NT):
                    PE.wait(th[s], *tok["z", s])
                    PE.quiet(lambda s=s: te.matmul(o, Mh[i][:, s, :], Zh[:, s, :], start=(s == 0), stop=False))
                    if full:
                        PE.quiet(lambda s=s: te.matmul(o, Mh[i][:, s, :], Zl[:, s, :], start=False, stop=False))
                        PE.wait(tl[s])
                        f = (lambda s=s: te.matmul(o, Ml[i][:, s, :], Zh[:, s, :], start=False, stop=(s == NT - 1)))
                    else:
                        f = (lambda s=s: te.matmul(o, Mh[i][:, s, :], Zl[:, s, :], start=False, stop=(s == NT - 1)))
                        if s == 0:
                            def extra():
                                with te.If(big["v"] > 0):
                                    for r in range(NT):
                                        te.matmul(o, Ml[i][:, r, :], Zh[:, r, :], start=False, stop=False)
                            zt = [tok["z", r] for r in range(NT)]
                            box["extra"] = (extra, zt)
                    if s < NT - 1 and signal:
                        tok["ms", s] = PE.op(f)
                    elif s < NT - 1:
                        PE.quiet(f)
                if "extra" in box:
                    PE.quiet(box["extra"][0], tl[0], *[w for z in box["extra"][1] for w in z])
                t = PE.op(f)
                if rowsum:
                    PE.wait(box["sum"], bank_free[7])
                    for c in (0, 1, 4):
                        ts = PE.op(lambda c=c: te.matmul(bank[7][0:T, 0:1], GW[0:T, d % 2, c * T:(c + 1) * T],
                                                         ones[0:T, 0:1], start=(c == 0), stop=(c == 4)))
                    box["ts"] = free["sum"][d % 2] = ts
                free["m"][i] = t
                if signal:
                    tok["ms", NT - 1] = t
                box["b"], box["t"] = b, t
            return mm

        def split_z(n, src, scale, *waits):
            sc = None if scale is None else scale[:, n:n + 1]
            if sc is None:
                th = A.op(lambda: ac.copy(Zh[:, n, :], src), *waits)
                tl = V.op(lambda: ve.tensor_tensor(Zl[:, n, :], src, Zh[:, n, :].bitcast(f32), ALU.subtract), th, *waits)
            else:
                th = A.op(lambda: ac.activation(Zh[:, n, :], src, ACT.Copy, scale=sc), *waits)
                tl = V.op(lambda: ve.scalar_tensor_tensor(Zl[:, n, :], src, sc, Zh[:, n, :].bitcast(f32), ALU.mult,
                                                         ALU.subtract), th, *waits)
            tok["z", n] = (th, tl)
            return tl, th

        def rsqrt(out, v, tmp, t):
            ti, to_ = tmp.bitcast(i32), out.bitcast(i32)
            t = V.op(lambda: ve.tensor_scalar(ti, v.bitcast(i32), 1, None, ALU.logical_shift_right), t)
            t = V.op(lambda: ve.tensor_scalar(to_, ti, -1.0, 1597463007.0, ALU.mult, ALU.add), t)
            for _ in range(3):
                t = P.op(lambda: po.tensor_tensor(tmp, out, out, ALU.mult), t)
                t = P.op(lambda: po.tensor_tensor(tmp, tmp, v, ALU.mult), t)
                t = P.op(lambda: po.tensor_scalar(tmp, tmp, -0.5, 1.5, ALU.mult, ALU.add), t)
                t = P.op(lambda: po.tensor_tensor(out, out, tmp, ALU.mult), t)
            return t

        def norm_stats(left, right, waits):
            i = nxt("st", 2)
            V.op(lambda: ve.bn_stats(st[i][:, 0:6], left), *waits, free["st"][i])
            t = V.op(lambda: ve.bn_stats(st[i][:, 6:12], right))
            t = V.op(lambda: ve.bn_aggr(mv[i][:, 0:2], st[i][:]), t)
            t = V.op(lambda: ve.tensor_scalar(mv[i][:, 2:3], mv[i][:, 1:2], 1e-5, None, ALU.add), t)
            return i, left, right, t

        def norm_apply(ln, t):
            i, left, right, _ = ln
            X = XO[i]
            ta = A.op(lambda: ac.activation(X[:, 0:HW], left, ACT.Identity, bias=mv[i][:, 5:6], scale=mv[i][:, 3:4]),
                      t, *free["xo"][i])
            tb = A.op(lambda: ac.activation(X[:, HW:D], right, ACT.Identity, bias=mv[i][:, 5:6], scale=mv[i][:, 3:4]))
            free["st"][i] = tb
            return ta, tb, i
        free["xo"] = [[], []]

        def transposes(src, parts, dst, t):
            done = []
            for g in range(parts // 4):
                bk = 6 + g
                PE.wait(bank_free[bk], t)
                for j in range(4):
                    tt = PE.op(lambda j=j, g=g, bk=bk: te.transpose(
                        bank[bk][:, j * T:(j + 1) * T], src[:, (4 * g + j) * 128:(4 * g + j + 1) * 128],
                        ident[0:T, 0:T]))
                v = bank[bk][:, 0:4 * T].rearrange("p (a c) -> p a c", c=T)
                ev = A.op(lambda g=g, v=v: ac.copy(XT[:, 4 * g:4 * g + 4, :], v), tt, free["xt"])
                bank_free[bk] = ev
                done.append(ev)
            w = s_xt.dma(A, ac, dst, XT[:, 0:parts, :], *done)
            free["xt"] = w
            return tt, w

        def pb_tile(col, d, bias, t):
            bk = 6 + d % 2
            PE.wait(t, bank_free[bk])
            tt = PE.op(lambda: te.matmul(bank[bk][0:T, 0:T], col[:, d:d + 1].to_broadcast([T, T]), ident[0:T, 0:T],
                                         start=True, stop=True))
            if bias is None:
                ev = A.op(lambda: ac.copy(PB[:, d, :], bank[bk][0:T, 0:T]), tt, free["pb"][d])
            else:
                ev = A.op(lambda: ac.activation(PB[:, d, :], bank[bk][0:T, 0:T], ACT.Identity, bias=bias), tt,
                          free["pb"][d])
            bank_free[bk] = ev
            tok["pb", d] = ev

        def finish_tile(job, d, layer):
            def soon(box):
                i, t = box["ln"][0], box["ln"][3]
                t = rsqrt(mv[i][:, 3:4], mv[i][:, 2:3], mv[i][:, 4:5], t)
                box["rstd"] = P.op(lambda: po.tensor_scalar(mv[i][:, 5:6], mv[i][:, 0:1], mv[i][:, 3:4], -1.0,
                                                            ALU.mult, ALU.mult), t)

            def mid(box):
                box["ln"] = ln = norm_apply(box["ln"], box["rstd"])
                free[box["hold"][0]][box["hold"][1]] = ln[1]
                box["extra"] = []

            def after_mid(box):
                ln = box["ln"]
                if layer == 1:
                    for j, col in ((0, PQ[0][1]), (1, PQ[0][0])):
                        box["extra"].append(V.op(lambda j=j, col=col: ve.tensor_tensor_reduce(
                            out=GS[:], in0=XO[ln[2]][:], in1=GW[0:T, j, :], scale=1.0, scalar=0.0, op0=ALU.mult,
                            op1=ALU.add, accum_out=col[:, d:d + 1]), ln[0], ln[1], tok["wal"], (V.sem, V.n)))
                    tok["pq", 0, d] = box["extra"][-1]

            def tail(box):
                ta, tb, i = box["ln"]
                if layer == 3:
                    free["xo"][i] = [s_xo[i].dma(A, ac, out[d * T:(d + 1) * T, :], XO[i][:], ta, tb)]
                    return
                if layer == 1:
                    pb_tile(PQ[0][1], d, None, tok["pq", 0, d])
                tt, w = transposes(XO[i], 8, xT_d[layer + 1][d].rearrange("p (k n) -> p k n", k=8), tb)
                s1 = s_xo[i].dma(A, ac, x_d[layer][d], XO[i][:], ta, tb)
                tok["xd", layer, d] = s1
                tok["xT", layer + 1, d] = w
                free["xo"][i] = [s1, tt] + box["extra"]
            job.soon, job.mid, job.after_mid, job.tail = soon, mid, after_mid, tail

        def gates(n, src, slot, *waits):
            for j, col in ((1, PQ[slot][1]), (0, PQ[slot][0])):
                t = V.op(lambda j=j, col=col: ve.tensor_tensor_reduce(
                    out=GS[:, 0:HW], in0=src, in1=GW[0:T, slot, j * HW:(j + 1) * HW], scale=1.0, scalar=0.0,
                    op0=ALU.mult, op1=ALU.add, accum_out=col[:, n:n + 1]), *waits, (V.sem, V.n))
            free["gw"][slot] = t
            tok["pq", slot, n] = t
            return t

        def load_gw(k):
            i = k % 2
            tok["gw", k] = s_gw[i].dma(S, sy, GW[:, i, :], gw[k].rearrange("c o -> o c").partition_broadcast(128)
                                       .rearrange("p o c -> p (o c)"), free["gw"][i])

        def add(job):
            jobs.append(job)
            return len(jobs) - 1

        s_g = [Slot(sem(f"s_g{i}")) for i in range(2)]

        def post_x1(n):
            def post(box):
                b, t = box["b"], box["t"]
                tg = V.op(lambda: ve.tensor_tensor(G[:, n, :], bank[b][0:T, :], B[0:T, :], ALU.add), t, tok["b"])
                give(b, tg)
                free["b"] = tg
                tok["yl", n] = s_g[n % 2].dma(S, sy, yl_d[n], G[:, n, :], tg, (s_g[n % 2].sem, s_g[n % 2].n))
                gates(n, G[:, n, :], 0, tok["gw", 0], tg)
                counts_out(n)
                split_z(n, G[:, n, :], DIS, tok["deg"], tg)
            return post

        load_b(b1)
        load_gw(0)
        load_gw(1)
        for b in range(NT):
            s_at.dma(A, ac, at_d[:, :, b * T:(b + 1) * T].rearrange("t p s -> p t s"),
                     AT[:, b, :].rearrange("p (t s) -> p t s", t=NT), tA)
        counts_float(0)
        degrees()
        for n in range(NT):
            late = (lambda box, n=n: counts_float(n + 1)) if n < NT - 1 else None
            if n < 2:
                mm, prep = (lambda box, n=n: (box.update(x_ahead[n]), mm_x(hW1)(box))[1]), (None, None, None)
            else:
                mm, prep = mm_x(hW1), prep_x(xT_d[0][n], lambda: ())
            add(Job(mm, prep, post_x1(n), w=hW1, late=late))
        add(Job(leave_build, after=len(jobs) - 1))

        s_w2 = [Slot(sem(f"s_w2{i}")) for i in range(2)]
        w2 = {"g": 0}

        def w2_step():
            g = w2["g"]
            if g == 16:
                return
            w2["g"] += 1
            h, k = divmod(g, 8)
            if k == 0:
                w2["a"] = [s_w2[j].dma(S, sy, UF[j][:], a2[0:1, j * D + h * HW:j * D + (h + 1) * HW]
                                       .partition_broadcast(128).rearrange("p o c -> p (o c)"), free["u"][j])
                           for j in range(2)]
            r = nxt("r", 4)
            t = s_r[r].dma(S, sy, RF[r][:], W2[k * 128:(k + 1) * 128, h * HW:(h + 1) * HW], free["r"][r])
            for j in range(2):
                t2 = V.op(lambda j=j: ve.tensor_tensor_reduce(
                    out=GS2[:], in0=RF[r][:], in1=UF[j][:], scale=1.0, scalar=0.0,
                    op0=ALU.mult, op1=ALU.add, accum_out=WP[:, h, j, k:k + 1]), t, w2["a"][j], (V.sem, V.n))
            free["r"][r] = free["u"][0] = free["u"][1] = t2
            if g == 15:
                tok["wc"] = V.op(lambda: ve.tensor_tensor(WC[:], WP[:, 0, :, :], WP[:, 1, :, :], ALU.add), t2)

        def bcast_job(col, bias=None):
            def mm(box):
                tpq = tok["pq", 0, NT - 1]
                box["ev"] = []
                for g, (u, w) in enumerate(((0, 4), (4, 8), (8, 10))):
                    b = take()
                    PE.wait(tpq, bank_free[b])
                    for k in range(u, w):
                        t = PE.op(lambda k=k, u=u, b=b: te.matmul(
                            bank[b][0:T, (k - u) * T:(k - u + 1) * T], col[:, k:k + 1].to_broadcast([T, T]),
                            ident[0:T, 0:T], start=True, stop=True))
                    v = bank[b][0:T, 0:(w - u) * T].rearrange("p (a c) -> p a c", c=T)
                    if bias is None:
                        ev = A.op(lambda u=u, w=w, v=v: ac.copy(PB[:, u:w, :], v), t)
                    else:
                        ev = A.op(lambda u=u, w=w, v=v: ac.activation(PB[:, u:w, :], v, ACT.Identity,
                                                                      bias=bias), t)
                    give(b, ev)
                for n in range(NT):
                    tok["pb", n] = ev
            return mm

        jb = add(Job(bcast_job(PQ[0][0], GB[0:T, 0:1]), after=len(jobs) - 1))
        ahead = None
        for k in range(4):
            nxt_box = {}
            for d in range(NT):
                load, first, second = prep_m("gate", d, k % 2, early=(k < 3))

                def load_w(box, k=k, load=load):
                    load_gw(k + 2)
                    load(box)

                def late(box, d=d):
                    box["r"] = [load_r(yl_d[d], tok["yl", d]), load_r(x[d * T:(d + 1) * T, 0:HW]),
                                load_r(x[d * T:(d + 1) * T, HW:D])]

                def pre(box, k=k, nb=nxt_box):
                    for n in range(7):
                        split_z(n, G[:, n, :], DIS, tok["ms", n], tok["g"])
                    build_part(nb, 0, (k + 1) % 2, 0)

                def post(box, d=d, k=k, nb=nxt_box):
                    b, t = box["b"], box["t"]
                    tg = V.op(lambda: ve.scalar_tensor_tensor(G[:, d, :], bank[b][0:T, :], DIS[:, d:d + 1], G[:, d, :],
                                                             ALU.mult, ALU.add), t, tok["deg"], *tok["z", d])
                    tok["g"] = tg
                    give(b, tg)
                    if k < 3:
                        box["pq"] = gates(d, G[:, d, :], (k + 1) % 2, tok["gw", k + 1], tg, free["pq"][(k + 1) % 2])
                        if d < NT - 1:
                            if d < NT - 2 and (d % 2 == 0 or k == 0):
                                w2_step()
                        else:
                            build_part(nb, 0, (k + 1) % 2, 1)
                            for n in range(7, NT):
                                split_z(n, G[:, n, :], DIS, tok["ms", n], tg)
                    else:
                        (r0, t0), (r1, t1), (r2, t2) = box["r"]
                        i = nxt("u", 2)
                        tl = V.op(lambda: ve.tensor_tensor(U[i][:], R[r1][:], R[r0][:], ALU.add), t1, t0,
                                  free["u"][i])
                        tr = V.op(lambda: ve.tensor_tensor(G[:, d, :], R[r2][:], G[:, d, :], ALU.add), t2, tg)
                        free["r"][r0] = free["r"][r1] = tl
                        free["r"][r2] = tr
                        box["hold"] = ("u", i)
                        box["ln"] = norm_stats(U[i][:], G[:, d, :], (tl, tr))

                def row(box, d=d, k=k):
                    pb_tile(PQ[(k + 1) % 2][0], d, GB[0:T, k + 1:k + 2], box["pq"])

                if d == 0 and k:
                    mm = (lambda box, nb=ahead, f=mm_m("gate"): (box.update(nb), f(box))[1])
                    job = Job(mm, post=post)
                    job.eager = True
                else:
                    job = Job(mm_m("gate", signal=(k < 3 and d == NT - 1)),
                              (load_w if d == 5 and k < 2 else load, first, second), post,
                              after=jb, after_post=last9 if k else -1)
                if k < 3:
                    job.tail = row
                    if d == NT - 1:
                        job.pre = pre
                else:
                    job.late = late
                    finish_tile(job, d, 0)
                j = add(job)
            last9 = j
            ahead = nxt_box

        pr2 = [dict() for _ in range(NT)]
        order = [("a", 0), ("a", 1), ("s", 0), ("s", 1), ("s", 2), ("s", 3)]
        for n in range(2, 8):
            order += [("a", n), ("s", n + 2)]
        order += [("a", 8), ("a", 9)]
        dep = [len(jobs) - NT + n for n in range(NT)]
        for l in range(2):
            src = xT_d[1] if l == 0 else hT_d
            bias = b0 if l == 0 else bb1
            if l == 0:
                rdy = lambda n: (tok["xT", 1, n],)
            else:
                rdy = lambda n: (tok["hT", 0, n], tok["hT", 1, n])
            done = {}
            for f in range(2):
                hZ = 1 + 4 * l + 2 * f
                hS = hZ + 1
                for n in range(NT):
                    def postz(box, n=n):
                        tl, th = split_z(n, bank[box["b"]][0:T, :], None, box["t"])
                        give(box["b"], tl)
                    add(Job(mm_x(hZ), prep_x(src[n], lambda n=n, r=rdy: r(n)), postz, after=dep[n], w=hZ))
                pair = [dict() for _ in range(NT)]
                for what, d in order:
                    def post(box, what=what, d=d, f=f, l=l, pair=pair):
                        pr = pair[d]
                        pr[what] = (box["b"], box["t"])
                        if len(pr) < 2:
                            return
                        (b, t), (b2, t2) = pr["a"], pr["s"]
                        i = nxt("u", 2)
                        tv = V.op(lambda: ve.scalar_tensor_tensor(U[i][:], bank[b][0:T, :], DEGI[:, d:d + 1], B[0:T, :],
                                                                 ALU.mult, ALU.add), t, tok["b"], free["u"][i])
                        give(b, tv)
                        free["b"] = tv
                        t1 = V.op(lambda: ve.tensor_tensor(U[i][:], U[i][:], bank[b2][0:T, :], ALU.add), t2, tv)
                        give(b2, t1)
                        if l == 0:
                            box["h"] = (i, A.op(lambda: ac.activation(U[i][:], U[i][:], ACT.Relu), t1))
                            return
                        r, tr = load_r(x_d[0][d][:, f * HW:(f + 1) * HW], tok["xd", 0, d]) if "r" not in pr2[d] \
                            else pr2[d].pop("r")
                        if f == 0:
                            t2 = V.op(lambda: ve.tensor_tensor(G[:, d, :], U[i][:], R[r][:], ALU.add), t1, tr)
                            free["u"][i] = free["r"][r] = t2
                        else:
                            t2 = V.op(lambda: ve.tensor_tensor(R[r][:], U[i][:], R[r][:], ALU.add), t1, tr)
                            free["u"][i] = t2
                            box["hold"] = ("r", r)
                            box["ln"] = norm_stats(G[:, d, :], R[r][:], (t2,))

                    second_one = (what == "a") == (d > 1)
                    if what == "a":
                        load, first, second = prep_m("mean", d)
                        if d == 0:
                            def load(box, load=load, bias=bias, f=f):
                                load_b(bias[f * HW:(f + 1) * HW])
                                load(box)
                        job = Job(mm_m("mean"), (load, first, second), post)
                    else:
                        job = Job(mm_x(hS), prep_x(src[d], lambda n=d, r=rdy: r(n)), post, w=hS)
                    if second_one:
                        if l == 0:
                            def tails(box, d=d, f=f):
                                i, t = box["h"]
                                tt, w = transposes(U[i], 4, hT_d[d].rearrange("p (k n) -> p k n", k=8)
                                                   [:, 4 * f:4 * f + 4, :], t)
                                tok["hT", f, d] = w
                                free["u"][i] = tt
                            job.tail = tails
                        else:
                            def late(box, d=d, f=f):
                                pr2[d]["r"] = load_r(x_d[0][d][:, f * HW:(f + 1) * HW], tok["xd", 0, d])
                            job.late = late
                            if f == 1:
                                finish_tile(job, d, 1)
                    j = add(job)
                    if second_one:
                        done[d] = j
                if l == 0 and f == 0:
                    def mmw(box):
                        for j in range(2):
                            for g in range(2):
                                b = take()
                                PE.wait(bank_free[b], tok["wc"])
                                for k in range(4):
                                    t = PE.op(lambda j=j, g=g, k=k, b=b: te.matmul(
                                        bank[b][:, k * 128:(k + 1) * 128],
                                        WC[:, j, 4 * g + k:4 * g + k + 1].to_broadcast([128, 128]), ident[:, :],
                                        start=True, stop=True))
                                ev = A.op(lambda j=j, g=g, b=b: ac.copy(GW[:, j, g * HW:(g + 1) * HW], bank[b][:]), t,
                                          free["gw"][0], free["gw"][1])
                                give(b, ev)
                        tok["wal"] = ev
                    add(Job(mmw))
            dep = [done[n] for n in range(NT)]

        base = 9
        prev_agg = []
        for f in range(2):
            hZ = base + f
            for n in range(NT):
                def postz(box, n=n):
                    tl, th = split_z(n, bank[box["b"]][0:T, :], None, box["t"])
                    give(box["b"], tl)
                add(Job(mm_x(hZ), prep_x(xT_d[2][n], lambda n=n: (tok["xT", 2, n],)), postz, after=dep[n], w=hZ))
            for d in range(NT):
                def late(box, d=d, f=f):
                    box["r"] = load_r(x_d[1][d][:, f * HW:(f + 1) * HW], tok["xd", 1, d])

                def post(box, d=d, f=f):
                    b, t = box["b"], box["t"]
                    r, tr = box["r"]
                    if f == 0:
                        q = V.op(lambda: ve.tensor_scalar(RS[:, d:d + 1], bank[7][0:T, 0:1], 1e-5, None, ALU.add), box["ts"])
                        bank_free[7] = q
                        tok["rs", d] = V.op(lambda: ve.reciprocal(RS[:, d:d + 1], RS[:, d:d + 1]), q)
                    i, j = nxt("u", 2), nxt("u", 2)
                    tv = V.op(lambda: ve.tensor_scalar(U[i][:], bank[b][0:T, :], RS[:, d:d + 1], None, ALU.mult), t,
                              tok["rs", d], free["u"][i])
                    give(b, tv)
                    tm = V.op(lambda: ve.tensor_scalar(U[j][:], U[i][:], 0.0, None, ALU.min), tv, free["u"][j])
                    te_ = A.op(lambda: ac.activation(U[j][:], U[j][:], ACT.Exp), tm)
                    t1 = V.op(lambda: ve.scalar_tensor_tensor(U[i][:], U[i][:], 0.0, U[j][:], ALU.max, ALU.add), te_)
                    free["u"][j] = t1
                    o = G[:, d, :] if f == 0 else R[r][:]
                    t2 = V.op(lambda: ve.scalar_tensor_tensor(o, U[i][:], -1.0, R[r][:], ALU.add, ALU.add), t1, tr)
                    free["u"][i] = t2
                    if f == 0:
                        free["r"][r] = t2
                    else:
                        box["hold"] = ("r", r)
                        box["ln"] = norm_stats(G[:, d, :], R[r][:], (t2,))
                kind = "kept" if f else "att"
                job = Job(mm_m(kind, d, rowsum=(f == 0)), prep_m(kind, d), post, after=dep[-1], late=late)
                if f == 1:
                    finish_tile(job, d, 2)
                j = add(job)
                if f == 1:
                    prev_agg.append(j)

        dep = prev_agg
        for f in range(2):
            hZ = 11 + f
            for n in range(NT):
                def postz(box, n=n):
                    tl, th = split_z(n, bank[box["b"]][0:T, :], D3, box["t"], tok["deg"])
                    give(box["b"], tl)
                add(Job(mm_x(hZ), prep_x(xT_d[3][n], lambda n=n: (tok["xT", 3, n],)), postz, after=dep[n], w=hZ))
            for d in range(NT):
                prep = prep_m("loop", d)
                if d == 0:
                    def load_first(box, f=f, load=prep[0]):
                        load_b(b3[f * HW:(f + 1) * HW])
                        load(box)
                    prep = (load_first,) + prep[1:]

                def late(box, d=d, f=f):
                    box["r"] = load_r(x_d[2][d][:, f * HW:(f + 1) * HW], tok["xd", 2, d])

                def post(box, d=d, f=f):
                    b, t = box["b"], box["t"]
                    r, tr = box["r"]
                    i = nxt("u", 2)
                    tv = V.op(lambda: ve.scalar_tensor_tensor(U[i][:], bank[b][0:T, :], D3[:, d:d + 1], B[0:T, :],
                                                             ALU.mult, ALU.add), t, tok["b"], free["u"][i])
                    give(b, tv)
                    free["b"] = tv
                    o = G[:, d, :] if f == 0 else R[r][:]
                    t2 = V.op(lambda: ve.scalar_tensor_tensor(o, U[i][:], 0.0, R[r][:], ALU.max, ALU.add), tv, tr)
                    free["u"][i] = t2
                    if f == 0:
                        free["r"][r] = t2
                    else:
                        box["hold"] = ("r", r)
                        box["ln"] = norm_stats(G[:, d, :], R[r][:], (t2,))
                job = Job(mm_m("loop"), prep, post, late=late)
                if f:
                    finish_tile(job, d, 3)
                add(job)

        box = [dict() for _ in jobs]
        first_use = {job.w: j for j, job in reversed(list(enumerate(jobs)))}
        w_left = -1
        final = {job.w: j for j, job in enumerate(jobs) if job.w is not None}
        at = {"post": -1, "load": 0, "first": 0, "second": 0, "tail": 0}

        def do_tails(upto):
            while at["tail"] <= upto:
                j = at["tail"]
                at["tail"] += 1
                if jobs[j].tail:
                    jobs[j].tail(box[j])

        def stage(name, upto, must, below):
            while at[name] <= min(upto, below - 1, len(jobs) - 1):
                j = at[name]
                if name == "load" and j > must and j - 1 > at["second"]:
                    return
                if name == "load" and jobs[j].after_post > at["post"]:
                    return
                if name == "load" and jobs[j].after >= at["tail"]:
                    if j > must:
                        return
                    do_tails(jobs[j].after)
                fn = {"load": jobs[j].load, "first": jobs[j].first, "second": jobs[j].second}[name]
                at[name] += 1
                if fn:
                    fn(box[j])

        n = len(jobs)
        for j, job in enumerate(jobs):
            stage("load", j, j, n)
            stage("first", j, j, n)
            stage("second", j, j, n)
            job.mm(box[j])
            if job.pre:
                job.pre(box[j])
            if job.eager:
                for s in ("load", "first", "second", "load"):
                    stage(s, j + 1 if s != "load" else at["load"], j + 1, n)
            do_tails(j - 3)
            stage("first", j + 2, j, at["load"])
            stage("load", j + 3, j, n)
            stage("first", j + 2, j, at["load"])
            stage("second", j + 2, j, at["first"])
            stage("load", j + 3, j, n)
            if j and jobs[j - 1].soon:
                jobs[j - 1].soon(box[j - 1])
            if j + 3 < n and jobs[j + 3].w is not None and final[jobs[j + 3].w] == j + 3 and jobs[j + 3].w < 12:
                stage_slabs(jobs[j + 3].w + 1)
            if j > 1 and jobs[j - 2].mid:
                jobs[j - 2].mid(box[j - 2])
            if j > 1 and jobs[j - 2].after_mid:
                jobs[j - 2].after_mid(box[j - 2])
            if job.late:
                job.late(box[j])
            if job.post:
                job.post(box[j])
            at["post"] = j
            if job.w is not None and final[job.w] == j:
                w_left = job.w
            may_load(w_left, j, first_use)
        do_tails(n - 3)
        jobs[n - 2].mid(box[n - 2])
        jobs[n - 1].soon(box[n - 1])
        jobs[n - 1].mid(box[n - 1])
        do_tails(n - 1)
        S.wait(*[(s.sem, s.n) for s in [s_xt, s_at] + s_xo + s_a + s_r + s_g + s_t])

        block = ctx.enter_context(nc.Block())
        for q, name in ((PE, "tensor"), (V, "vector"), (A, "scalar"), (P, "gpsimd"), (S, "sync")):
            def body(eng, q=q):
                q.emit(eng)
            {"tensor": block.tensor, "vector": block.vector, "scalar": block.scalar, "gpsimd": block.gpsimd,
             "sync": block.sync}[name](body)


_OUTS = [((N, D), "float32")]


def kernel(**inputs):
    import numpy as _np
    import concourse.bacc as _bacc
    from concourse import mybir as _mybir
    from concourse.bass_utils import run_bass_kernel_spmd as _run

    nc = _bacc.Bacc("TRN2", target_bir_lowering=False, num_devices=1)
    get = {k: _np.asarray(v) for k, v in inputs.items()}
    x = get["x"]
    win = _np.array([[lo * T for lo, hi in windows()], [(hi + 1) * T - 1 for lo, hi in windows()]], _np.float32)
    win = _np.tile(win.reshape(1, 2 * NC), (T, 1))
    arrays = {
        "xT": x.reshape(NT, T, 8, 128).transpose(0, 3, 2, 1).reshape(NT, 128, 8 * T),
        "x": x,
        "es": get["src"].reshape(NC, T).T,
        "ed": get["dst"].reshape(NC, T).T,
        "win": win,
        "W1": get["L0_gnn_W1"], "b1": get["L0_gnn_b1"], "gw": get["L0_gnn_gate_w"], "gb": get["L0_gnn_gate_b"],
        "Ws0": get["L1_gnn_W_self0"], "Wn0": get["L1_gnn_W_neigh0"], "b0": get["L1_gnn_b0"],
        "Ws1": get["L1_gnn_W_self1"], "Wn1": get["L1_gnn_W_neigh1"], "bb1": get["L1_gnn_b1"],
        "W2": get["L2_gnn_W"], "a2": get["L2_gnn_a"], "W3": get["L3_gnn_W"], "b3": get["L3_gnn_b"],
    }
    args, named = [], {}
    for name, a in arrays.items():
        a = _np.ascontiguousarray(a)
        named[f"in_{name}"] = a
        args.append(nc.dram_tensor(f"in_{name}", a.shape, _mybir.dt.from_np(a.dtype), kind="ExternalInput").ap())
    o = nc.dram_tensor("out_0", _OUTS[0][0], _mybir.dt.float32, kind="ExternalOutput").ap()
    gnn_program(nc, *args, o)
    r = _run(nc, [named], core_ids=[0])
    return r.results[0]["out_0"]
```
